# Optimizing a Trainium2 kernel written in Bass

```python
import numpy as np
import jax
import jax.numpy as jnp

def _softmax(x, axis=-1):
    return jax.nn.softmax(x, axis=axis)

def _gelu(x):
    return jax.nn.gelu(x, approximate=True)

def _silu(x):
    return jax.nn.silu(x)

def _sigmoid(x):
    return jax.nn.sigmoid(x)

def _layernorm(x, axis=-1, eps=1e-05):
    m = jnp.mean(x, axis=axis, keepdims=True)
    v = jnp.var(x, axis=axis, keepdims=True)
    return (x - m) / jnp.sqrt(v + eps)

def _scatter_add(tgt, idx, src, axis=0):
    return tgt.at[idx].add(src)

def _segment_sum(src, seg, n):
    return jax.ops.segment_sum(src, seg, n)
kernel_name = 'mk_metaformer_d1_conv_nchw512_r4_27f5c6'

def setup_inputs(seed: int=0):
    np.random.seed(seed)
    _w = jnp.asarray

    def _rec_inputs():
        import jax
        import jax.numpy as jnp
        _gk = jax.random.key(seed)
        x = 1.648e-05 + 1 * jax.random.normal(jax.random.fold_in(_gk, 1), (8, 128, 48, 48), jnp.float32)
        return x
    x = _rec_inputs()

    def _L0_conv_setup():
        import jax, jax.numpy as jnp
        import numpy as np
        HEADS = 8
        EMBED = 128

        def _feature(t):
            return jax.nn.elu(t) + 1.0

        def _to_multihead(t, heads):
            n, c, h, w = t.shape
            t = t.reshape(n, heads, c // heads, h * w)
            return jnp.transpose(t, (0, 1, 3, 2))

        def _linear_causal_numerator(Q, K, V):
            n, heads, L, dk = Q.shape
            dv = V.shape[-1]
            Qs = jnp.moveaxis(Q, 2, 0)
            Ks = jnp.moveaxis(K, 2, 0)
            Vs = jnp.moveaxis(V, 2, 0)
            S0 = jnp.zeros((n, heads, dk, dv), Q.dtype)

            def step(S, qkv):
                q, k, v = qkv
                S = S + k[..., :, None] * v[..., None, :]
                o = jnp.einsum('nhk,nhkv->nhv', q, S)
                return (S, o)
            _, outs = jax.lax.scan(step, S0, (Qs, Ks, Vs))
            return jnp.moveaxis(outs, 0, 2)
        key = jax.random.key(seed)
        k0, k1, k2 = jax.random.split(key, 3)
        x = jax.random.normal(k0, (8, 128, 48, 48), dtype=jnp.float32)
        scale = 1.0 / np.sqrt(512.0)
        Wq = jax.random.normal(k1, (128, 128), dtype=jnp.float32) * scale
        bq = jnp.zeros((128,), dtype=jnp.float32)
        Wkv = jax.random.normal(k2, (256, 128), dtype=jnp.float32) * scale
        bkv = jnp.zeros((256,), dtype=jnp.float32)
        return {'x': x, 'Wq': Wq, 'bq': bq, 'Wkv': Wkv, 'bkv': bkv}
    _L0_conv_all = _L0_conv_setup()
    _L0_conv_in = {k: v for k, v in _L0_conv_all.items() if k in ('Wq', 'bq', 'Wkv', 'bkv')}
    del _L0_conv_all

    def _L0_ffn_setup():
        import jax, jax.numpy as jnp
        import numpy as np
        B, C, IN_LEN, OUT_LEN, E, TOP_K, N_I = (1, 2048, 128, 128, 8, 2, 16)
        key = jax.random.key(seed)
        ks = jax.random.split(key, 8)
        w = lambda k, shape, sc=0.02: jax.random.normal(k, shape, dtype=jnp.float32) * sc
        return {'x': jax.random.normal(ks[0], (B, C, IN_LEN), dtype=jnp.float32), 'Ins_tk': jax.random.normal(ks[1], (B, N_I, OUT_LEN), dtype=jnp.float32), 'gate_w': w(ks[2], (IN_LEN, E)), 'expert_w': w(ks[3], (E, IN_LEN, OUT_LEN)), 'expert_b': jnp.zeros((E, OUT_LEN), dtype=jnp.float32), 'gamma_w': w(ks[4], (E, OUT_LEN)), 'beta_w': w(ks[5], (E, OUT_LEN, OUT_LEN)), 'rmod_w': w(ks[6], (OUT_LEN, E))}
    _L0_ffn_all = _L0_ffn_setup()
    _L0_ffn_in = {k: v for k, v in _L0_ffn_all.items() if k in ('Ins_tk', 'gate_w', 'expert_w', 'expert_b', 'gamma_w', 'beta_w', 'rmod_w')}
    del _L0_ffn_all
    return {'x': x, 'L0_conv_Wq': _L0_conv_in['Wq'], 'L0_conv_bq': _L0_conv_in['bq'], 'L0_conv_Wkv': _L0_conv_in['Wkv'], 'L0_conv_bkv': _L0_conv_in['bkv'], 'L0_ffn_Ins_tk': _L0_ffn_in['Ins_tk'], 'L0_ffn_gate_w': _L0_ffn_in['gate_w'], 'L0_ffn_expert_w': _L0_ffn_in['expert_w'], 'L0_ffn_expert_b': _L0_ffn_in['expert_b'], 'L0_ffn_gamma_w': _L0_ffn_in['gamma_w'], 'L0_ffn_beta_w': _L0_ffn_in['beta_w'], 'L0_ffn_rmod_w': _L0_ffn_in['rmod_w']}

def reference(x, L0_conv_Wq, L0_conv_bq, L0_conv_Wkv, L0_conv_bkv, L0_ffn_Ins_tk, L0_ffn_gate_w, L0_ffn_expert_w, L0_ffn_expert_b, L0_ffn_gamma_w, L0_ffn_beta_w, L0_ffn_rmod_w):
    import jax
    import jax.numpy as jnp

    def _L0_conv_ref(x, Wq, bq, Wkv, bkv):
        import jax, jax.numpy as jnp
        import numpy as np
        HEADS = 8
        EMBED = 128

        def _feature(t):
            return jax.nn.elu(t) + 1.0

        def _to_multihead(t, heads):
            n, c, h, w = t.shape
            t = t.reshape(n, heads, c // heads, h * w)
            return jnp.transpose(t, (0, 1, 3, 2))

        def _linear_causal_numerator(Q, K, V):
            n, heads, L, dk = Q.shape
            dv = V.shape[-1]
            Qs = jnp.moveaxis(Q, 2, 0)
            Ks = jnp.moveaxis(K, 2, 0)
            Vs = jnp.moveaxis(V, 2, 0)
            S0 = jnp.zeros((n, heads, dk, dv), Q.dtype)

            def step(S, qkv):
                q, k, v = qkv
                S = S + k[..., :, None] * v[..., None, :]
                o = jnp.einsum('nhk,nhkv->nhv', q, S)
                return (S, o)
            _, outs = jax.lax.scan(step, S0, (Qs, Ks, Vs))
            return jnp.moveaxis(outs, 0, 2)
        n, _, h, w = x.shape
        q = jnp.einsum('nchw,oc->nohw', x, Wq) + bq[None, :, None, None]
        kv = jnp.einsum('nchw,oc->nohw', x, Wkv) + bkv[None, :, None, None]
        K_, V_ = (kv[:, :EMBED], kv[:, EMBED:])
        Q = _feature(_to_multihead(q, HEADS))
        K = _feature(_to_multihead(K_, HEADS))
        V = _to_multihead(V_, HEADS)
        den = 1.0 / (jnp.einsum('nhld,nhld->nhl', Q, jnp.cumsum(K, axis=1)) + 1e-10)
        num = _linear_causal_numerator(Q, K, V)
        out = num * den[..., None]
        out = jnp.transpose(out, (0, 1, 3, 2)).reshape(n, -1, h, w)
        return out

    def _L0_ffn_ref(x, Ins_tk, gate_w, expert_w, expert_b, gamma_w, beta_w, rmod_w):
        import jax, jax.numpy as jnp
        import numpy as np
        B, C, IN_LEN, OUT_LEN, E, TOP_K, N_I = (1, 2048, 128, 128, 8, 2, 16)
        Bx, Cx, L = x.shape
        xf = x.reshape(-1, L)
        ins = Ins_tk[0]
        router_gamma = jnp.mean(ins @ rmod_w, axis=0)
        logits = xf @ gate_w + router_gamma
        probs = jax.nn.softmax(logits.astype(jnp.float32), axis=-1)
        rw, sel = jax.lax.top_k(probs, TOP_K)
        combine = jnp.sum(jax.nn.one_hot(sel, E, dtype=rw.dtype) * rw[..., None], axis=1)
        gam = jnp.mean(ins @ gamma_w.T, axis=0)
        bet = jnp.einsum('nh,ehd->ed', ins, beta_w) / N_I
        eo = jnp.einsum('nl,eld->end', xf, expert_w) + expert_b[:, None, :]
        mod = gam[:, None, None] * eo + bet[:, None, :]
        out = jnp.einsum('ne,end->nd', combine, mod)
        return out.reshape(Bx, Cx, OUT_LEN)

    def _gn(v, G=32, eps=1e-05):
        B_, C_, H_, W_ = v.shape
        g = v.reshape(B_, G, C_ // G, H_, W_)
        m = jnp.mean(g, axis=(2, 3, 4), keepdims=True)
        s = jnp.var(g, axis=(2, 3, 4), keepdims=True)
        return ((g - m) / jnp.sqrt(s + eps)).reshape(v.shape)

    def _ln_c(v, eps=1e-06):
        m = jnp.mean(v, axis=1, keepdims=True)
        s = jnp.var(v, axis=1, keepdims=True)
        return (v - m) / jnp.sqrt(s + eps)

    def _ln_t(v, eps=1e-05):
        m = jnp.mean(v, axis=-1, keepdims=True)
        s = jnp.var(v, axis=-1, keepdims=True)
        return (v - m) / jnp.sqrt(s + eps)

    def _to_tokens(v):
        B_, C_, H_, W_ = v.shape
        return v.reshape(B_, C_, H_ * W_).transpose(0, 2, 1)

    def _from_tokens(t, like):
        B_, C_, H_, W_ = like.shape
        return t.transpose(0, 2, 1).reshape(B_, C_, H_, W_)
    x = x + _L0_conv_ref(_ln_c(x), L0_conv_Wq, L0_conv_bq, L0_conv_Wkv, L0_conv_bkv)
    t = _to_tokens(x)
    t = t + _L0_ffn_ref(_ln_t(t), L0_ffn_Ins_tk, L0_ffn_gate_w, L0_ffn_expert_w, L0_ffn_expert_b, L0_ffn_gamma_w, L0_ffn_beta_w, L0_ffn_rmod_w)
    x = _from_tokens(t, x)
    return x

_drawn_inputs = setup_inputs


def setup_inputs(seed=0):
    import zlib

    import numpy as np

    out = dict(_drawn_inputs(seed))
    spreads = {'L0_conv_bq': (0.0, 0.8), 'L0_conv_bkv': (0.0, 0.1), 'L0_ffn_expert_b': (0.0, 2.0)}
    factors = {'L0_ffn_Ins_tk': 8.0,
     'L0_ffn_gate_w': 8.0,
     'L0_ffn_expert_w': 8.0,
     'L0_ffn_gamma_w': 8.0,
     'L0_ffn_beta_w': 8.0,
     'L0_ffn_rmod_w': 8.0}
    for name, (base, spread) in spreads.items():
        noise = np.random.default_rng([zlib.crc32(name.encode()), seed]).standard_normal(out[name].shape)
        drawn = base * np.exp(spread * noise) if base else spread * noise
        out[name] = jnp.asarray(drawn.astype(out[name].dtype))
    for name, factor in factors.items():
        out[name] = (out[name] * factor).astype(out[name].dtype)
    return out
```

```python
from contextlib import ExitStack

import concourse.bass as bass
from concourse import mybir

F32 = mybir.dt.float32
ALU = mybir.AluOpType
ACT = mybir.ActivationFunctionType
AX = mybir.AxisListType.X

IMAGES, CH, TOKENS = 8, 128, 48 * 48
HEADS, HD = 8, 16
EXPERTS, INSTR = 8, 16
T = 128
U = 4
CHUNKS = TOKENS // T
PAR = IMAGES // U
GROUPS = PAR * CHUNKS
PAIRS = HEADS // 2
HALF_U = U // 2
BIG = 1.0e30

WEIGHTS = 12
CONSTS = 3 + EXPERTS + 6
SETUP_DVE = 1 + 2 + 1 + 3 + 6 + EXPERTS + 1
POOL_A = 1 + HEADS
POOL_C = 1
POOL_Y = 2 * U
DVE_A = 3
DVE_C = 1 + 15
DVE_Y = 3 * U


class Group:

    def __init__(self, half, par):
        self.half, self.par, self.i = half, par, half * PAR + par


def program(nc, x_d, wq_d, bq_d, wkv_d, bkv_d, ins_d, gate_d, ew_d, eb_d, gamma_d, beta_d, rmod_d, out_d):
    ctx = ExitStack()
    with ctx:
        def sb(name, shape):
            return ctx.enter_context(nc.sbuf_tensor(name, shape, F32))

        def ps(name):
            return ctx.enter_context(nc.psum_tensor(name, [128, 512], F32))

        def sem(name):
            return ctx.enter_context(nc.semaphore(name))

        ident = sb("ident", [128, 128])
        tri = sb("tri", [128, T])
        heads_mask = sb("heads_mask", [128, 128])
        parity = sb("parity", [128, 2])
        order = sb("order", [128, U, EXPERTS])
        centre = sb("centre", [128, 128])
        mean_ins = sb("mean_ins", [INSTR, 128])
        minus_half = sb("minus_half", [128, U])
        w_raw = sb("w_raw", [128, 3, 128])
        w_t = sb("w_t", [128, 384])
        w_qkv = sb("w_qkv", [128, 384])
        b_qkv = sb("b_qkv", [128, 384])
        gate_raw = sb("gate_raw", [128, EXPERTS])
        gate_w = sb("gate_w", [128, EXPERTS])
        rmod = sb("rmod", [128, EXPERTS])
        router_b = sb("router_b", [128, EXPERTS])
        ins = sb("ins", [INSTR, 128])
        ins_mean = sb("ins_mean", [128, 128])
        gamma_raw = sb("gamma_raw", [EXPERTS, 128])
        gamma_t = sb("gamma_t", [128, EXPERTS])
        gamma_all = sb("gamma_all", [128, EXPERTS])
        gamma_col = sb("gamma_col", [EXPERTS, 1])
        beta_raw = sb("beta_raw", [128, EXPERTS, 128])
        beta_t = sb("beta_t", [128, EXPERTS])
        e_bias_raw = sb("e_bias_raw", [EXPERTS, 128])
        e_bias = sb("e_bias", [EXPERTS, 128])
        e_raw = sb("e_raw", [128, EXPERTS, 128])
        e_w = sb("e_w", [128, EXPERTS, 128])
        pause = sb("pause", [128, 1])
        eps = sb("eps", [128, 2, U])
        x = sb("x", [128, PAR, U, T])
        bn = sb("bn", [128, U, 6])
        mv1 = sb("mv1", [128, PAR, U, 2])
        ve1 = sb("ve1", [128, U])
        rstd1 = sb("rstd1", [128, PAR, U])
        qkv = sb("qkv", [128, PAR, U, 384])
        ex = sb("ex", [128, U, 256])
        feat = sb("feat", [128, PAR, U, 256])
        k_sum = sb("k_sum", [128, U, HEADS, HD])
        qk = sb("qk", [128, U, 128])
        den = sb("den", [128, U, HEADS])
        rden = sb("rden", [128, U, HEADS])
        qn = sb("qn", [128, U, 128])
        v_pad = sb("v_pad", [128, PAR, U, HEADS, 32])
        k_even = sb("k_even", [128, PAR, U, T])
        k_odd = sb("k_odd", [128, PAR, U, T])
        q_t = sb("q_t", [128, PAR, U, T])
        probs = sb("probs", [128, 2, PAIRS, HALF_U, 2, T])
        kv_new = sb("kv_new", [128, U, 128])
        state = sb("state", [128, IMAGES, 128])
        x1 = sb("x1", [128, PAR, U, T])
        bn2 = sb("bn2", [128, U, 6])
        mv2 = sb("mv2", [128, PAR, U, 2])
        ve2 = sb("ve2", [128, U])
        rstd2 = sb("rstd2", [128, PAR, U])
        lg0 = sb("lg0", [128, U, EXPERTS])
        lg = sb("lg", [128, U, EXPERTS])
        lgm = sb("lgm", [128, U, EXPERTS])
        lg2 = sb("lg2", [128, U, EXPERTS])
        top = sb("top", [128, 4, U])
        rank = sb("rank", [128, 2, U, EXPERTS])
        hot = sb("hot", [128, 3, U, EXPERTS])
        pexp = sb("pexp", [128, U, EXPERTS])
        psum_ = sb("psum_", [128, 2, U])
        psel = sb("psel", [128, U, EXPERTS])
        coef = sb("coef", [128, PAR, U, EXPERTS])
        scale = sb("scale", [128, PAR, U, EXPERTS])
        y_act = sb("y_act", [128, 2, 4, 128])
        y_dve = sb("y_dve", [128, 2, 128])
        y_sum = sb("y_sum", [128, 2, 128])
        y = sb("y", [128, PAR, U, 128])
        coef_t = sb("coef_t", [EXPERTS, PAR, U * T])
        o = sb("o", [128, PAR, U, T])

        big = [ps(f"big{n}") for n in range(4)]
        bank_t = ps("bank_t")
        bank_p = ps("bank_p")
        bank_q = ps("bank_q")
        bank_n = ps("bank_n")

        names = ("consts setup w_loaded setup_pe setup_dve "
                 "xt_done stats1_done rstd1_done proj_done qkv_done ex_done feat_done v_pad_done qk_done "
                 "den_done qn_done kt_done k_evac qt_done q_evac "
                 "score_done prob_done kv_done kv_evac state_done inter_done pv_done x1_done "
                 "x1t_done logit_done stats2_done rstd2_done lg_read lgm_done pexp_done coef_done scale_done "
                 "y_done y_act_done y_dve_done y_sum_done ct_done ct_evac out_done o_done "
                 "dve_a dve_c dve_y pool_a pool_c pool_y").split()
        S = {n: sem(n) for n in names}
        x_loaded = [sem(f"x_loaded{b}") for b in range(PAR)]
        stored = [sem(f"stored{b}") for b in range(PAR)]

        def dram(d, g):
            return d[U * g.par:U * g.par + U, :, bass.ds(g.half * T, T)].rearrange("n p t -> p n t")

        def need(eng, name, count):
            if not isinstance(count, int) or count > 0:
                eng.wait_ge(S[name], count)

        def steps(eng, step):
            def grp(n):
                return Group(n // PAR, n % PAR) if 0 <= n < GROUPS else None

            first, last = 2, CHUNKS - 1
            for k in range(-1, PAR * first):
                step(grp(k + 1), grp(k), grp(k - 1), grp(k - 2))
            with eng.Fori(first, last) as t:
                step(Group(t, 1), Group(t, 0), Group(t - 1, 1), Group(t - 1, 0))
                step(Group(t + 1, 0), Group(t, 1), Group(t, 0), Group(t - 1, 1))
            for k in range(PAR * last, GROUPS + 2):
                step(grp(k + 1), grp(k), grp(k - 1), grp(k - 2))

        block = ctx.enter_context(nc.Block())

        @block.sync
        def _(sp):
            def load(g):
                if not isinstance(g.i, int) or g.i >= PAR:
                    need(sp, "x1_done", g.i - PAR + 1)
                sp.dma_start(x[:, g.par], dram(x_d, g)).then_inc(x_loaded[g.par], 16)

            load(Group(0, 0))
            weights = [
                (w_raw[:, 0], wq_d), (w_raw[:, 1], wkv_d[0:128]), (w_raw[:, 2], wkv_d[128:256]),
                (b_qkv[:, 0:128], bq_d.partition_broadcast(128)),
                (b_qkv[:, 128:384], bkv_d.partition_broadcast(128)),
                (gate_raw[:], gate_d), (rmod[:], rmod_d), (ins[:], ins_d[0]), (gamma_raw[:], gamma_d),
                (e_bias_raw[:], eb_d), (beta_raw[:], beta_d.rearrange("e h d -> h e d")),
                (e_raw[:], ew_d.rearrange("e l d -> l e d")),
            ]
            assert len(weights) == WEIGHTS
            for dst, src in weights:
                sp.dma_start(dst, src).then_inc(S["w_loaded"], 16)
            load(Group(0, 1))

            def step(a, b, c, d):
                if d:
                    need(sp, "o_done", d.i + 1)
                    sp.dma_start(dram(out_d, d), o[:, d.par]).then_inc(stored[d.par], 16)
                if b:
                    ahead = Group(b.half + 1, b.par)
                    if not isinstance(ahead.i, int) or ahead.i < GROUPS:
                        load(ahead)

            steps(sp, step)
            for b in range(PAR):
                sp.wait_ge(stored[b], 16 * CHUNKS)

        @block.gpsimd
        def _(pool):
            nc.gpsimd.memset(ident[:], 0.0).then_inc(S["setup"], 1)
            nc.gpsimd.memset(tri[:], 1.0).then_inc(S["setup"], 1)
            nc.gpsimd.memset(heads_mask[:], 1.0).then_inc(S["setup"], 1)
            pool.wait_ge(S["setup"], 3)
            nc.gpsimd.affine_select(out=ident[:], in_=ident[:], compare_op=ALU.not_equal, fill=1.0, base=0,
                                    pattern=[[-1, 128]], channel_multiplier=1).then_inc(S["consts"], 1)
            nc.gpsimd.affine_select(out=tri[:], in_=tri[:], compare_op=ALU.is_ge, fill=0.0, base=0,
                                    pattern=[[1, T]], channel_multiplier=-1).then_inc(S["consts"], 1)
            blocks = heads_mask[:].rearrange("p (h d) -> p h d", d=HD)
            nc.gpsimd.affine_select(out=blocks, in_=blocks, compare_op=ALU.is_ge, fill=0.0, base=0,
                                    pattern=[[-HD, HEADS], [0, HD]], channel_multiplier=1).then_inc(S["setup"], 1)
            pool.wait_ge(S["setup"], 4)
            nc.gpsimd.affine_select(out=blocks, in_=blocks, compare_op=ALU.is_ge, fill=0.0, base=HD - 1,
                                    pattern=[[HD, HEADS], [0, HD]], channel_multiplier=-1).then_inc(S["consts"], 1)
            for e in range(EXPERTS):
                nc.gpsimd.memset(order[:, :, e:e + 1], float(EXPERTS - e)).then_inc(S["consts"], 1)
            nc.gpsimd.memset(mean_ins[:], 1.0 / INSTR).then_inc(S["consts"], 1)
            nc.gpsimd.memset(minus_half[:], -0.5).then_inc(S["consts"], 1)
            nc.gpsimd.memset(eps[:, 0], 1e-6).then_inc(S["consts"], 1)
            nc.gpsimd.memset(eps[:, 1], 1e-5).then_inc(S["consts"], 1)
            nc.gpsimd.memset(v_pad[:], 0.0).then_inc(S["consts"], 1)
            nc.gpsimd.memset(state[:], 0.0).then_inc(S["consts"], 1)
            pool.wait_ge(S["consts"], CONSTS)

            def step(a, b, c, d):
                if a:
                    p, n = a.par, a.i
                    need(pool, "stats1_done", n + 1)
                    nc.gpsimd.tensor_tensor(ve1[:], mv1[:, p, :, 1], eps[:, 0], ALU.add)\
                        .then_inc(S["pool_a"], 1)
                    need(pool, "pool_a", POOL_A * n + 1)
                    nc.gpsimd.tensor_tensor(rstd1[:, p], ve1[:], minus_half[:], ALU.pow).then_inc(S["rstd1_done"], 1)
                if c:
                    p, n = c.par, c.i
                    need(pool, "stats2_done", n + 1)
                    nc.gpsimd.tensor_tensor(ve2[:], mv2[:, p, :, 1], eps[:, 1], ALU.add)\
                        .then_inc(S["pool_c"], 1)
                    need(pool, "pool_c", POOL_C * n + 1)
                    need(pool, "scale_done", n - PAR + 1)
                    nc.gpsimd.tensor_tensor(rstd2[:, p], ve2[:], minus_half[:], ALU.pow).then_inc(S["rstd2_done"], 1)
                if a:
                    p, n = a.par, a.i
                    f = feat[:, p].rearrange("p u (s h d) -> p u s h d", s=2, d=HD)
                    need(pool, "feat_done", 2 * (n + 1))
                    need(pool, "pv_done", 2 * (n - 1))
                    nc.gpsimd.tensor_tensor(k_sum[:, :, 1], f[:, :, 1, 0], f[:, :, 1, 1], ALU.add)\
                        .then_inc(S["pool_a"], 1)
                    nc.gpsimd.tensor_copy(k_sum[:, :, 0], f[:, :, 1, 0]).then_inc(S["pool_a"], 1)
                    for e in range(2):
                        v = qkv[:, p, :, 256:384].rearrange("p u (g e d) -> p u g e d", e=2, d=HD)[:, :, :, e]
                        nc.gpsimd.tensor_copy(v_pad[:, p, :, e::2, HD * e:HD * e + HD], v)\
                            .then_inc(S["v_pad_done"], 1)
                    for h in range(2, HEADS):
                        need(pool, "pool_a", POOL_A * n + 1 + h)
                        nc.gpsimd.tensor_tensor(k_sum[:, :, h], k_sum[:, :, h - 1], f[:, :, 1, h], ALU.add)\
                            .then_inc(S["pool_a"], 1)
                    need(pool, "pool_a", POOL_A * (n + 1))
                    need(pool, "den_done", n)
                    nc.gpsimd.tensor_tensor(qk[:], k_sum[:].rearrange("p u h d -> p u (h d)"),
                                            feat[:, p, :, 0:128], ALU.mult).then_inc(S["qk_done"], 1)
                if c:
                    sum_experts(c, 0)
                    sum_experts(c, 1)
                if b:
                    p, n = b.par, b.i
                    need(pool, "kv_evac", n + 1)
                    need(pool, "inter_done", n + 1)
                    mine = state[:, U * p:U * p + U]
                    nc.gpsimd.tensor_tensor(mine, mine, kv_new[:], ALU.add).then_inc(S["state_done"], 1)
                if a:
                    p, n = a.par, a.i
                    need(pool, "den_done", n + 1)
                    need(pool, "qt_done", n)
                    nc.gpsimd.tensor_tensor(qn[:].rearrange("p u (h d) -> p u h d", d=HD),
                                            feat[:, p, :, 0:128].rearrange("p u (h d) -> p u h d", d=HD),
                                            rden[:].unsqueeze(3).broadcast_to([128, U, HEADS, HD]), ALU.mult)\
                        .then_inc(S["qn_done"], 1)
                if c:
                    sum_experts(c, 2)
                    sum_experts(c, 3)

            def sum_experts(c, u):
                n, s = c.i, u % 2
                need(pool, "y_act_done", U * n + u + 1)
                if u == 0:
                    need(pool, "out_done", n - 1)
                nc.gpsimd.tensor_tensor(y_act[:, s, 0:2], y_act[:, s, 0:2], y_act[:, s, 2:4], ALU.add)\
                    .then_inc(S["pool_y"], 1)
                need(pool, "pool_y", POOL_Y * n + 2 * u + 1)
                nc.gpsimd.tensor_tensor(y_sum[:, s], y_act[:, s, 0], y_act[:, s, 1], ALU.add)\
                    .then_inc(S["pool_y"], 1)
                need(pool, "pool_y", POOL_Y * n + 2 * u + 2)
                need(pool, "y_dve_done", U * n + u + 1)
                nc.gpsimd.tensor_tensor(y[:, c.par, u], y_sum[:, s], y_dve[:, s], ALU.add)\
                    .then_inc(S["y_sum_done"], 1)

            steps(pool, step)

        @block.scalar
        def _(act):
            def expert_products(c, u):
                n, s = c.i, u % 2
                need(act, "y_done", 2 * (U * n + u) + 1)
                need(act, "y_sum_done", U * n + u - 1)
                for e in range(4):
                    last = nc.scalar.activation(y_act[:, s, e], big[2 * s][:, 128 * e:128 * e + 128], ACT.Copy,
                                                scale=scale[:, c.par, u, e:e + 1])
                last.then_inc(S["y_act_done"], 1)

            def step(a, b, c, d):
                for h in range(2):
                    if a:
                        need(act, "qkv_done", U * a.i + HALF_U * (h + 1))
                        need(act, "feat_done", 2 * (a.i - 1) + h + 1)
                        nc.scalar.activation(ex[:, 2 * h:2 * h + 2], qkv[:, a.par, 2 * h:2 * h + 2, 0:256], ACT.Exp,
                                             bias=-1.0).then_inc(S["ex_done"], 1)
                    if c and h == 0:
                        need(act, "lgm_done", c.i + 1)
                        need(act, "coef_done", c.i)
                        nc.scalar.activation(pexp[:], lgm[:], ACT.Exp).then_inc(S["pexp_done"], 1)
                if c:
                    need(act, "scale_done", c.i + 1)
                    expert_products(c, 0)
                    expert_products(c, 1)
                if a:
                    p, n = a.par, a.i
                    need(act, "kt_done", n + 1)
                    need(act, "score_done", 8 * (n - 1))
                    for e, dst in ((0, k_even), (1, k_odd)):
                        nc.scalar.activation(dst[:, p].rearrange("p u t -> p (u t)"), bank_t[:], ACT.Copy,
                                             scale=parity[:, e:e + 1]).then_inc(S["k_evac"], 1)
                if c:
                    expert_products(c, 2)
                    expert_products(c, 3)
                    need(act, "ct_done", c.i + 1)
                    need(act, "out_done", c.i - 1)
                    nc.scalar.activation(coef_t[:, c.par], bank_p[0:EXPERTS, :], ACT.Copy).then_inc(S["ct_evac"], 1)
                if a:
                    need(act, "qt_done", a.i + 1)
                    need(act, "inter_done", a.i - 1)
                    nc.scalar.activation(q_t[:, a.par].rearrange("p u t -> p (u t)"), bank_q[:], ACT.Copy)\
                        .then_inc(S["q_evac"], 1)

            act.wait_ge(S["setup_dve"], SETUP_DVE)
            steps(act, step)

        @block.vector
        def _(dve):
            done = [0]

            def setup(instruction):
                instruction.then_inc(S["setup_dve"], 1)
                done[0] += 1

            tt, stt = nc.vector.tensor_tensor, nc.vector.scalar_tensor_tensor
            dve.wait_ge(S["consts"], CONSTS)
            setup(nc.vector.tensor_scalar(centre[:], ident[:], -1.0 / CH, None, ALU.add))
            for e in range(2):
                first = heads_mask[:].rearrange("p (g e d) -> p e g d", e=2, d=HD)[:, e, :, 0]
                setup(nc.vector.reduce_sum(parity[:, e:e + 1], first, axis=AX))
            dve.wait_ge(S["w_loaded"], 16 * WEIGHTS)
            setup(nc.vector.tensor_scalar(b_qkv[:, 0:256], b_qkv[:, 0:256], 1.0, None, ALU.add))
            dve.wait_ge(S["setup_pe"], 1)
            setup(nc.vector.tensor_copy(w_t[:], bank_t[:, 0:384]))
            setup(nc.vector.tensor_copy(gamma_t[:], bank_p[:, 0:EXPERTS]))
            setup(nc.vector.tensor_copy(ins_mean[:], bank_q[:, 0:128]))
            dve.wait_ge(S["setup_pe"], 2)
            setup(nc.vector.tensor_copy(w_qkv[:], bank_t[:, 0:384]))
            setup(nc.vector.tensor_copy(gate_w[:], bank_p[:, 0:EXPERTS]))
            setup(nc.vector.tensor_copy(gamma_all[:], bank_q[:, 0:EXPERTS]))
            setup(nc.vector.tensor_copy(router_b[:], bank_n[:, 0:EXPERTS]))
            setup(nc.vector.tensor_copy(beta_t[:], big[2][:, 0:EXPERTS]))
            setup(nc.vector.tensor_copy(gamma_col[:], big[3][0:EXPERTS, 0:1]))
            dve.wait_ge(S["setup_dve"], done[0])
            for e in range(EXPERTS):
                setup(nc.vector.tensor_scalar(e_w[:, e], big[e // 4][:, 128 * (e % 4):128 * (e % 4) + 128],
                                              gamma_all[:, e:e + 1], None, ALU.mult))
            dve.wait_ge(S["setup_pe"], 3)
            setup(stt(e_bias[:], e_bias_raw[:], gamma_col[:], bank_t[0:EXPERTS, 0:128], ALU.mult, ALU.add))
            assert done[0] == SETUP_DVE
            dve.wait_ge(S["setup_dve"], SETUP_DVE)

            def stats(bank, parts, out, chain, count):
                for u in range(U):
                    last = nc.vector.bn_stats(parts[:, u], bank[:, T * u:T * u + T])
                last.then_inc(S[chain], 1)
                need(dve, chain, count)
                nc.vector.memset(pause[:], 0.0)
                for u in range(U):
                    last = nc.vector.bn_aggr(out[:, u], parts[:, u])
                return last

            def causal(b, half):
                need(dve, "pv_done", 2 * (b.i - 1) + half + 1)
                for g in range(PAIRS):
                    need(dve, "score_done", 8 * b.i + 4 * half + g + 1)
                    tt(probs[:, half, g].rearrange("p u e t -> p (u e) t"),
                       big[g][:].rearrange("p (n t) -> p n t", t=T),
                       tri[:].unsqueeze(1).broadcast_to([128, 2 * HALF_U, T]), ALU.mult).then_inc(S["prob_done"], 1)

            def project(a, u):
                need(dve, "proj_done", U * a.i + u + 1)
                stt(qkv[:, a.par, u], (bank_p, bank_q)[u % 2][:, 0:384], rstd1[:, a.par, u:u + 1], b_qkv[:],
                    ALU.mult, ALU.add).then_inc(S["qkv_done"], 1)

            def features(a, h):
                need(dve, "ex_done", 2 * a.i + h + 1)
                stt(feat[:, a.par, 2 * h:2 * h + 2], ex[:, 2 * h:2 * h + 2], 1.0,
                    qkv[:, a.par, 2 * h:2 * h + 2, 0:256], ALU.min, ALU.max).then_inc(S["feat_done"], 1)

            def per_token(v):
                return v.unsqueeze(2).broadcast_to([128, U, EXPERTS])

            def route(c, n):
                p = c.par
                if n > 0:
                    need(dve, "dve_c", DVE_C * c.i + 1 + n)
                if n == 0:
                    need(dve, "logit_done", c.i + 1)
                    need(dve, "rstd2_done", c.i + 1)
                    i = tt(lg0[:], bank_p[:, 0:U * EXPERTS].rearrange("p (u e) -> p u e", u=U),
                           per_token(rstd2[:, p]), ALU.mult)
                    i.then_inc(S["lg_read"], 1)
                    need(dve, "lg_read", c.i + 1)
                    i = tt(lg[:], lg0[:], router_b[:].unsqueeze(1).broadcast_to([128, U, EXPERTS]), ALU.add)
                elif n == 1:
                    i = nc.vector.reduce_max(top[:, 0], lg[:], axis=AX)
                elif n == 2:
                    need(dve, "pexp_done", c.i)
                    i = tt(lgm[:], lg[:], per_token(top[:, 0]), ALU.subtract)
                    i.then_inc(S["lgm_done"], 1)
                    need(dve, "lgm_done", c.i + 1)
                    i = stt(rank[:, 0], lgm[:], 0.0, order[:], ALU.is_ge, ALU.mult)
                elif n == 3:
                    i = nc.vector.reduce_max(top[:, 1], rank[:, 0], axis=AX)
                elif n == 4:
                    i = tt(hot[:, 0], rank[:, 0], per_token(top[:, 1]), ALU.is_equal)
                elif n == 5:
                    i = stt(lg2[:], hot[:, 0], -BIG, lgm[:], ALU.mult, ALU.add)
                elif n == 6:
                    i = nc.vector.reduce_max(top[:, 2], lg2[:], axis=AX)
                elif n == 7:
                    i = tt(rank[:, 1], lg2[:], per_token(top[:, 2]), ALU.is_equal)
                elif n == 8:
                    i = tt(lg0[:], rank[:, 1], order[:], ALU.mult)
                elif n == 9:
                    i = nc.vector.reduce_max(top[:, 3], lg0[:], axis=AX)
                elif n == 10:
                    i = tt(hot[:, 1], lg0[:], per_token(top[:, 3]), ALU.is_equal)
                elif n == 11:
                    i = tt(hot[:, 2], hot[:, 0], hot[:, 1], ALU.add)
                elif n == 12:
                    need(dve, "pexp_done", c.i + 1)
                    i = nc.vector.reduce_sum(psum_[:, 0], pexp[:], axis=AX)
                elif n == 13:
                    i = nc.vector.reciprocal(psum_[:, 1], psum_[:, 0])
                elif n == 14:
                    i = tt(psel[:], pexp[:], hot[:, 2], ALU.mult)
                elif n == 15:
                    need(dve, "ct_done", c.i - 1)
                    tt(coef[:, p], psel[:], per_token(psum_[:, 1]), ALU.mult).then_inc(S["coef_done"], 1)
                    need(dve, "coef_done", c.i + 1)
                    need(dve, "y_act_done", U * (c.i - 1))
                    tt(scale[:, p], coef[:, p], per_token(rstd2[:, p]), ALU.mult).then_inc(S["scale_done"], 1)
                    return
                i.then_inc(S["dve_c"], 1)

            def weigh_experts(c, first):
                need(dve, "scale_done", c.i + 1)
                for e in range(4):
                    for u in (first, first + 1):
                        s = u % 2
                        out = big[2 * s + 1][:, 128 * e:128 * e + 128]
                        w = scale[:, c.par, u, 4 + e:5 + e]
                        if e == 0:
                            need(dve, "y_done", 2 * (U * c.i + u) + 2)
                            need(dve, "y_sum_done", U * c.i + u - 1)
                            i = nc.vector.tensor_scalar(y_dve[:, s], out, w, None, ALU.mult)
                        else:
                            need(dve, "dve_y", DVE_Y * c.i + 3 * first + 2 * (e - 1) + s + 1)
                            i = stt(y_dve[:, s], out, w, y_dve[:, s], ALU.mult, ALU.add)
                        i.then_inc(S["y_dve_done" if e == 3 else "dve_y"], 1)

            def step(a, b, c, d):
                if c:
                    need(dve, "x1t_done", c.i + 1)
                    stats(bank_n, bn2, mv2[:, c.par], "dve_c", DVE_C * c.i + 1).then_inc(S["stats2_done"], 1)
                if b:
                    causal(b, 0)
                if a:
                    need(dve, "xt_done", a.i + 1)
                    stats(bank_t, bn, mv1[:, a.par], "dve_a", DVE_A * a.i + 1).then_inc(S["stats1_done"], 1)
                if c:
                    route(c, 0)
                    route(c, 1)
                    route(c, 2)
                if d:
                    need(dve, "out_done", d.i + 1)
                    if not isinstance(d.half, int) or d.half > 0:
                        dve.wait_ge(stored[d.par], 16 * d.half)
                    tt(o[:, d.par].rearrange("p u t -> p (u t)"), bank_q[:],
                       x1[:, d.par].rearrange("p u t -> p (u t)"), ALU.add).then_inc(S["o_done"], 1)
                if a:
                    need(dve, "rstd1_done", a.i + 1)
                    need(dve, "kv_done", a.i - 1)
                    need(dve, "v_pad_done", 2 * (a.i - 1))
                for u in range(U):
                    if a:
                        project(a, u)
                    if c:
                        for n in range(3 + 3 * u, 6 + 3 * u if u < 3 else 16):
                            route(c, n)
                if b:
                    need(dve, "kv_done", b.i + 1)
                    need(dve, "state_done", b.i)
                    tt(kv_new[:], bank_p[:].rearrange("p (u d) -> p u d", u=U),
                       heads_mask[:].unsqueeze(1).broadcast_to([128, U, 128]), ALU.mult).then_inc(S["kv_evac"], 1)
                if a:
                    need(dve, "qn_done", a.i - 1)
                    features(a, 0)
                    features(a, 1)
                if c:
                    weigh_experts(c, 0)
                if b:
                    causal(b, 1)
                if a:
                    need(dve, "qk_done", a.i + 1)
                    nc.vector.reduce_sum(den[:], qk[:].rearrange("p u (h d) -> p u h d", d=HD), axis=AX)\
                        .then_inc(S["dve_a"], 1)
                    need(dve, "dve_a", DVE_A * a.i + 2)
                    nc.vector.tensor_scalar(den[:], den[:], 1e-10, None, ALU.add).then_inc(S["dve_a"], 1)
                    need(dve, "dve_a", DVE_A * a.i + 3)
                    need(dve, "qn_done", a.i)
                    nc.vector.reciprocal(rden[:], den[:]).then_inc(S["den_done"], 1)
                if c:
                    weigh_experts(c, 2)
                if b:
                    need(dve, "pv_done", 2 * (b.i + 1))
                    need(dve, "y_done", 8 * (b.i - 1))
                    tt(x1[:, b.par].rearrange("p u t -> p (u t)"), bank_n[:],
                       x[:, b.par].rearrange("p u t -> p (u t)"), ALU.add).then_inc(S["x1_done"], 1)

            steps(dve, step)

        @block.tensor
        def _(pe):
            mm, transpose = nc.tensor.matmul, nc.tensor.transpose
            pe.wait_ge(S["consts"], CONSTS)
            pe.wait_ge(S["w_loaded"], 16 * WEIGHTS)
            for n in range(3):
                transpose(bank_t[:, 128 * n:128 * n + 128], w_raw[:, n], ident[:])
            transpose(bank_p[:, 0:EXPERTS], gamma_raw[:], ident[0:EXPERTS, 0:EXPERTS])
            mm(bank_q[:, 0:128], ins[:], mean_ins[:], start=True, stop=True).then_inc(S["setup_pe"], 1)
            pe.wait_ge(S["setup_dve"], 7)
            mm(bank_t[:, 0:384], centre[:], w_t[:], start=True, stop=True)
            mm(bank_p[:, 0:EXPERTS], centre[:], gate_raw[:], start=True, stop=True)
            mm(bank_q[:, 0:EXPERTS], ins_mean[:], gamma_t[:], start=True, stop=True)
            mm(bank_n[:, 0:EXPERTS], ins_mean[:], rmod[:], start=True, stop=True)
            for n in range(2):
                mm(big[n][:], centre[:], e_raw[:, 4 * n:4 * n + 4], start=True, stop=True)
            for e in range(EXPERTS):
                mm(big[2][:, e:e + 1], beta_raw[:, e], ins_mean[:, 0:1], start=True, stop=True)
            mm(big[3][0:EXPERTS, 0:1], gamma_t[:], ins_mean[:, 0:1], start=True, stop=True)\
                .then_inc(S["setup_pe"], 1)
            pe.wait_ge(S["setup_dve"], SETUP_DVE - 1)
            transpose(bank_t[0:EXPERTS, 0:128], beta_t[:], ident[:]).then_inc(S["setup_pe"], 1)
            pe.wait_ge(S["setup_dve"], SETUP_DVE)

            def scores(b, half):
                p = b.par
                for g in range(PAIRS):
                    rows = slice(32 * g, 32 * g + 32)
                    for v in range(HALF_U):
                        u = HALF_U * half + v
                        for e, k in ((0, k_even), (1, k_odd)):
                            at = T * (2 * v + e)
                            last = mm(big[g][:, at:at + T], k[rows, p, u], q_t[rows, p, u], start=True, stop=True)
                    last.then_inc(S["score_done"], 1)

            def values(b, half):
                p = b.par
                need(pe, "prob_done", 8 * b.i + 4 * (half + 1))
                for v in range(HALF_U):
                    u = HALF_U * half + v
                    for e in range(2):
                        for g in range(PAIRS):
                            last = mm(bank_n[32 * g:32 * g + 32, T * u:T * u + T], v_pad[:, p, u, 2 * g + e],
                                      probs[:, half, g, v, e], start=False, stop=(e == 1), skip_group_check=True)
                last.then_inc(S["pv_done"], 1)

            def project(a, u):
                mm((bank_p, bank_q)[u % 2][:, 0:384], x[:, a.par, u], w_qkv[:], start=True, stop=True)\
                    .then_inc(S["proj_done"], 1)

            def experts(b, c, u):
                for half in range(2):
                    bank = 2 * (u % 2) + half
                    if b:
                        need(pe, "prob_done", 8 * b.i + 4 * (u // 2) + bank + 1)
                    elif half == 0:
                        need(pe, "y_act_done", U * c.i + u - 1)
                    else:
                        need(pe, "y_dve_done", U * c.i + u - 1)
                    mm(big[bank][:], x1[:, c.par, u], e_w[:, 4 * half:4 * half + 4], start=True, stop=True)\
                        .then_inc(S["y_done"], 1)

            def step(a, b, c, d):
                if c:
                    p, n = c.par, c.i
                    need(pe, "x1_done", n + 1)
                    for u in range(U):
                        last = transpose(bank_n[:, T * u:T * u + T], x1[:, p, u], ident[:])
                    last.then_inc(S["x1t_done"], 1)
                    need(pe, "ct_evac", n)
                    for u in range(U):
                        last = mm(bank_p[:, EXPERTS * u:EXPERTS * (u + 1)], x1[:, p, u], gate_w[:],
                                  start=True, stop=True)
                    last.then_inc(S["logit_done"], 1)
                if b:
                    need(pe, "k_evac", 2 * (b.i + 1))
                    need(pe, "q_evac", b.i + 1)
                    need(pe, "y_act_done", U * (b.i - 1))
                    need(pe, "y_dve_done", U * (b.i - 1))
                    need(pe, "prob_done", 8 * b.i)
                    scores(b, 0)
                if a:
                    p, n = a.par, a.i
                    pe.wait_ge(x_loaded[p], 16 * (a.half + 1))
                    need(pe, "k_evac", 2 * n)
                    for u in range(U):
                        last = transpose(bank_t[:, T * u:T * u + T], x[:, p, u], ident[:])
                    last.then_inc(S["xt_done"], 1)
                if d:
                    p, n = d.par, d.i
                    need(pe, "y_sum_done", U * (n + 1))
                    need(pe, "ct_evac", n + 1)
                    if not b:
                        need(pe, "o_done", n)
                    mm(bank_q[:], e_bias[:], coef_t[:, p], start=True, stop=False, skip_group_check=True)
                    for u in range(U):
                        last = mm(bank_q[:, T * u:T * u + T], y[:, p, u], ident[:], start=False, stop=(u == U - 1),
                                  skip_group_check=True)
                    last.then_inc(S["out_done"], 1)
                if a:
                    if c:
                        need(pe, "lg_read", c.i + 1)
                    else:
                        need(pe, "qkv_done", U * a.i - 1)
                    project(a, 0)
                    if d:
                        need(pe, "o_done", d.i + 1)
                    project(a, 1)
                if b:
                    p, n = b.par, b.i
                    if c:
                        need(pe, "stats2_done", c.i + 1)
                    need(pe, "state_done", n - 1)
                    for u in range(U):
                        last = mm(bank_n[:, T * u:T * u + T], state[:, U * p + u], q_t[:, p, u],
                                  start=(u == 0), stop=False, skip_group_check=True)
                    last.then_inc(S["inter_done"], 1)
                if a:
                    need(pe, "qkv_done", U * a.i + 1)
                    project(a, 2)
                    need(pe, "qkv_done", U * a.i + 2)
                    project(a, 3)
                if c:
                    experts(b, c, 0)
                    experts(b, c, 1)
                if b:
                    p, n = b.par, b.i
                    if a:
                        need(pe, "qkv_done", U * a.i + 3)
                    else:
                        need(pe, "lg_read", c.i + 1)
                    for u in range(U):
                        last = mm(bank_p[:, 128 * u:128 * u + 128], feat[:, p, u, 128:256], qkv[:, p, u, 256:384],
                                  start=True, stop=True)
                    last.then_inc(S["kv_done"], 1)
                    need(pe, "v_pad_done", 2 * (n + 1))
                    values(b, 0)
                    if c:
                        need(pe, "y_act_done", U * c.i + 2)
                        need(pe, "y_dve_done", U * c.i + 2)
                    scores(b, 1)
                if a:
                    p, n = a.par, a.i
                    need(pe, "feat_done", 2 * (n + 1))
                    for u in range(U):
                        last = transpose(bank_t[:, T * u:T * u + T], feat[:, p, u, 128:256], ident[:])
                    last.then_inc(S["kt_done"], 1)
                if c:
                    experts(b, c, 2)
                    experts(b, c, 3)
                    need(pe, "coef_done", c.i + 1)
                    if b:
                        need(pe, "kv_evac", b.i + 1)
                    else:
                        need(pe, "lg_read", c.i + 1)
                    for u in range(U):
                        last = transpose(bank_p[0:EXPERTS, T * u:T * u + T], coef[:, c.par, u], ident[:])
                    last.then_inc(S["ct_done"], 1)
                if a:
                    p, n = a.par, a.i
                    need(pe, "qn_done", n + 1)
                    need(pe, "qkv_done", U * (n + 1))
                    for u in range(U):
                        last = transpose(bank_q[:, T * u:T * u + T], qn[:, u], ident[:])
                    last.then_inc(S["qt_done"], 1)
                if b:
                    values(b, 1)

            steps(pe, step)


_NAMES = ["x", "L0_conv_Wq", "L0_conv_bq", "L0_conv_Wkv", "L0_conv_bkv", "L0_ffn_Ins_tk", "L0_ffn_gate_w",
          "L0_ffn_expert_w", "L0_ffn_expert_b", "L0_ffn_gamma_w", "L0_ffn_beta_w", "L0_ffn_rmod_w"]


def kernel(**inputs):
    import numpy as np
    import concourse.bacc as bacc
    from concourse.bass_utils import run_bass_kernel_spmd

    nc = bacc.Bacc("TRN2", target_bir_lowering=False, num_devices=1)
    arrays, args = {}, []
    for name in _NAMES:
        a = np.ascontiguousarray(inputs[name])
        if name == "x":
            a = a.reshape(IMAGES, CH, TOKENS)
        arrays["in_" + name] = a
        args.append(nc.dram_tensor("in_" + name, a.shape, mybir.dt.from_np(a.dtype), kind="ExternalInput").ap())
    out = nc.dram_tensor("out", (IMAGES, CH, TOKENS), F32, kind="ExternalOutput").ap()
    program(nc, *args, out)
    result = run_bass_kernel_spmd(nc, [arrays], core_ids=[0])
    return result.results[0]["out"].reshape(IMAGES, CH, 48, 48)
```

```python
from contextlib import ExitStack

import concourse.bass as bass
from concourse import mybir

F32 = mybir.dt.float32
F32R = mybir.dt.float32r
ALU = mybir.AluOpType
ACT = mybir.ActivationFunctionType
AX = mybir.AxisListType.X

IMAGES, CH, TOKENS = 8, 128, 48 * 48
HEADS, HD = 8, 16
EXPERTS, INSTR = 8, 16
T = 128
U = 4
CHUNKS = TOKENS // T
PAR = IMAGES // U
GROUPS = PAR * CHUNKS
PAIRS = HEADS // 2
HALF_U = U // 2
BIG = 1.0e30

WEIGHTS = 12
CONSTS = 3 + EXPERTS + 6
SETUP_DVE = 1 + 2 + 1 + 3 + 6 + EXPERTS + 2 + 1
POOL_A = HEADS
POOL_C = 1
POOL_Y = 2 * U
DVE_A = 2
DVE_C = 1 + 15
DVE_Y = 3 * U


class Group:

    def __init__(self, half, par):
        self.half, self.par, self.i = half, par, half * PAR + par


def program(nc, x_d, wq_d, bq_d, wkv_d, bkv_d, ins_d, gate_d, ew_d, eb_d, gamma_d, beta_d, rmod_d, out_d):
    ctx = ExitStack()
    with ctx:
        def sb(name, shape, dtype=F32):
            return ctx.enter_context(nc.sbuf_tensor(name, shape, dtype))

        def ps(name):
            return ctx.enter_context(nc.psum_tensor(name, [128, 512], F32))

        def sem(name):
            return ctx.enter_context(nc.semaphore(name))

        ident = sb("ident", [128, 128])
        tri = sb("tri", [128, T])
        heads_mask = sb("heads_mask", [128, 128])
        parity = sb("parity", [128, 2])
        order = sb("order", [128, U, EXPERTS])
        centre = sb("centre", [128, 128])
        mean_ins = sb("mean_ins", [INSTR, 128])
        minus_half = sb("minus_half", [128, U])
        w_raw = sb("w_raw", [128, 3, 128])
        w_t = sb("w_t", [128, 384])
        w_qkv = sb("w_qkv", [128, 384])
        b_qkv = sb("b_qkv", [128, 384])
        gate_raw = sb("gate_raw", [128, EXPERTS])
        gate_w = sb("gate_w", [128, EXPERTS])
        rmod = sb("rmod", [128, EXPERTS])
        router_b = sb("router_b", [128, EXPERTS])
        ins = sb("ins", [INSTR, 128])
        ins_mean = sb("ins_mean", [128, 128])
        gamma_raw = sb("gamma_raw", [EXPERTS, 128])
        gamma_t = sb("gamma_t", [128, EXPERTS])
        gamma_all = sb("gamma_all", [128, EXPERTS])
        gamma_col = sb("gamma_col", [EXPERTS, 1])
        beta_raw = sb("beta_raw", [128, EXPERTS, 128])
        beta_t = sb("beta_t", [128, EXPERTS])
        e_bias_raw = sb("e_bias_raw", [EXPERTS, 128])
        e_bias = sb("e_bias", [EXPERTS, 128])
        e_raw = sb("e_raw", [128, EXPERTS, 128])
        e_w = sb("e_w", [128, EXPERTS, 128])
        e_high = sb("e_high", [128, EXPERTS, 128], F32R)
        e_low = sb("e_low", [128, EXPERTS, 128], F32R)
        pause = sb("pause", [128, 1])
        eps = sb("eps", [128, 2, U])
        x = sb("x", [128, PAR, U, T])
        x_res = sb("x_res", [128, PAR, U, T])
        bn = sb("bn", [128, U, 6])
        mv1 = sb("mv1", [128, PAR, U, 2])
        ve1 = sb("ve1", [128, U])
        rstd1 = sb("rstd1", [128, PAR, U])
        qkv = sb("qkv", [128, PAR, U, 384])
        ex = sb("ex", [128, U, 256])
        feat = sb("feat", [128, PAR, U, 256])
        k_sum = sb("k_sum", [128, U, HEADS, HD])
        qk = sb("qk", [128, U, 128])
        den = sb("den", [128, U, HEADS])
        rden = sb("rden", [128, U, HEADS])
        qn = sb("qn", [128, U, 128])
        v_pad = sb("v_pad", [128, PAR, U, HEADS, 32])
        k_even = sb("k_even", [128, PAR, U, T])
        k_odd = sb("k_odd", [128, PAR, U, T])
        q_t = sb("q_t", [128, PAR, U, T])
        probs = sb("probs", [128, 2, PAIRS, HALF_U, 2, T])
        kv_new = sb("kv_new", [128, U, 128])
        state = sb("state", [128, IMAGES, 128])
        x1 = sb("x1", [128, PAR, U, T])
        x1_high = sb("x1_high", [128, PAR, U, T], F32R)
        x1_low = sb("x1_low", [128, PAR, U, T], F32R)
        bn2 = sb("bn2", [128, U, 6])
        mv2 = sb("mv2", [128, PAR, U, 2])
        ve2 = sb("ve2", [128, U])
        rstd2 = sb("rstd2", [128, PAR, U])
        lg0 = sb("lg0", [128, U, EXPERTS])
        lg = sb("lg", [128, U, EXPERTS])
        lgm = sb("lgm", [128, U, EXPERTS])
        lg2 = sb("lg2", [128, U, EXPERTS])
        top = sb("top", [128, 4, U])
        rank = sb("rank", [128, 2, U, EXPERTS])
        hot = sb("hot", [128, 3, U, EXPERTS])
        pexp = sb("pexp", [128, U, EXPERTS])
        psum_ = sb("psum_", [128, 2, U])
        psel = sb("psel", [128, U, EXPERTS])
        coef = sb("coef", [128, PAR, U, EXPERTS])
        scale = sb("scale", [128, PAR, U, EXPERTS])
        y_act = sb("y_act", [128, 2, 4, 128])
        y_dve = sb("y_dve", [128, 2, 128])
        y_sum = sb("y_sum", [128, 2, 128])
        y = sb("y", [128, PAR, U, 128])
        coef_t = sb("coef_t", [EXPERTS, PAR, U * T])
        o = sb("o", [128, PAR, U, T])

        big = [ps(f"big{n}") for n in range(4)]
        bank_t = ps("bank_t")
        bank_p = ps("bank_p")
        bank_q = ps("bank_q")
        bank_n = ps("bank_n")

        names = ("consts setup w_loaded setup_pe setup_dve "
                 "xt_done x_res_done stats1_done rstd1_done proj_done qkv_done ex_done feat_done v_pad_done qk_done "
                 "den_done qn_done kt_done k_evac qt_done q_evac "
                 "score_done prob_done kv_done kv_evac state_done inter_done pv_done x1_done "
                 "x1t_done high_done low_done logit_done stats2_done rstd2_done lg_read lgm_done pexp_done coef_done scale_done "
                 "y_done y_act_done y_dve_done y_sum_done ct_done ct_evac out_done o_done "
                 "dve_s dve_a dve_c dve_y pool_s pool_a pool_c pool_y").split()
        S = {n: sem(n) for n in names}
        x_loaded = [sem(f"x_loaded{b}") for b in range(PAR)]
        stored = [sem(f"stored{b}") for b in range(PAR)]

        def dram(d, g):
            return d[U * g.par:U * g.par + U, :, bass.ds(g.half * T, T)].rearrange("n p t -> p n t")

        def need(eng, name, count):
            if not isinstance(count, int) or count > 0:
                eng.wait_ge(S[name], count)

        def steps(eng, step):
            def grp(n):
                return Group(n // PAR, n % PAR) if 0 <= n < GROUPS else None

            first, last = 2, CHUNKS - 2
            for k in range(-2, PAR * first):
                step(grp(k + 2), grp(k + 1), grp(k), grp(k - 1), grp(k - 2))
            with eng.Fori(first, last) as t:
                step(Group(t + 1, 0), Group(t, 1), Group(t, 0), Group(t - 1, 1), Group(t - 1, 0))
                step(Group(t + 1, 1), Group(t + 1, 0), Group(t, 1), Group(t, 0), Group(t - 1, 1))
            for k in range(PAR * last, GROUPS + 2):
                step(grp(k + 2), grp(k + 1), grp(k), grp(k - 1), grp(k - 2))

        block = ctx.enter_context(nc.Block())

        @block.sync
        def _(sp):
            def load(g):
                need(sp, "proj_done", U * (g.i - PAR + 1))
                need(sp, "x_res_done", g.i - PAR + 1)
                sp.dma_start(x[:, g.par], dram(x_d, g)).then_inc(x_loaded[g.par], 16)

            load(Group(0, 0))
            weights = [
                (w_raw[:, 0], wq_d), (w_raw[:, 1], wkv_d[0:128]), (w_raw[:, 2], wkv_d[128:256]),
                (b_qkv[:, 0:128], bq_d.partition_broadcast(128)),
                (b_qkv[:, 128:384], bkv_d.partition_broadcast(128)),
                (gate_raw[:], gate_d), (rmod[:], rmod_d), (ins[:], ins_d[0]), (gamma_raw[:], gamma_d),
                (e_bias_raw[:], eb_d), (beta_raw[:], beta_d.rearrange("e h d -> h e d")),
                (e_raw[:], ew_d.rearrange("e l d -> l e d")),
            ]
            assert len(weights) == WEIGHTS
            for dst, src in weights:
                sp.dma_start(dst, src).then_inc(S["w_loaded"], 16)
            load(Group(0, 1))

            def step(s, a, b, c, d):
                if d:
                    need(sp, "o_done", d.i + 1)
                    sp.dma_start(dram(out_d, d), o[:, d.par]).then_inc(stored[d.par], 16)
                if a:
                    ahead = Group(a.half + 1, a.par)
                    if not isinstance(ahead.i, int) or ahead.i < GROUPS:
                        load(ahead)

            steps(sp, step)
            for b in range(PAR):
                sp.wait_ge(stored[b], 16 * CHUNKS)

        @block.gpsimd
        def _(pool):
            nc.gpsimd.memset(ident[:], 0.0).then_inc(S["setup"], 1)
            nc.gpsimd.memset(tri[:], 1.0).then_inc(S["setup"], 1)
            nc.gpsimd.memset(heads_mask[:], 1.0).then_inc(S["setup"], 1)
            pool.wait_ge(S["setup"], 3)
            nc.gpsimd.affine_select(out=ident[:], in_=ident[:], compare_op=ALU.not_equal, fill=1.0, base=0,
                                    pattern=[[-1, 128]], channel_multiplier=1).then_inc(S["consts"], 1)
            nc.gpsimd.affine_select(out=tri[:], in_=tri[:], compare_op=ALU.is_ge, fill=0.0, base=0,
                                    pattern=[[1, T]], channel_multiplier=-1).then_inc(S["consts"], 1)
            blocks = heads_mask[:].rearrange("p (h d) -> p h d", d=HD)
            nc.gpsimd.affine_select(out=blocks, in_=blocks, compare_op=ALU.is_ge, fill=0.0, base=0,
                                    pattern=[[-HD, HEADS], [0, HD]], channel_multiplier=1).then_inc(S["setup"], 1)
            pool.wait_ge(S["setup"], 4)
            nc.gpsimd.affine_select(out=blocks, in_=blocks, compare_op=ALU.is_ge, fill=0.0, base=HD - 1,
                                    pattern=[[HD, HEADS], [0, HD]], channel_multiplier=-1).then_inc(S["consts"], 1)
            for e in range(EXPERTS):
                nc.gpsimd.memset(order[:, :, e:e + 1], float(EXPERTS - e)).then_inc(S["consts"], 1)
            nc.gpsimd.memset(mean_ins[:], 1.0 / INSTR).then_inc(S["consts"], 1)
            nc.gpsimd.memset(minus_half[:], -0.5).then_inc(S["consts"], 1)
            nc.gpsimd.memset(eps[:, 0], 1e-6).then_inc(S["consts"], 1)
            nc.gpsimd.memset(eps[:, 1], 1e-5).then_inc(S["consts"], 1)
            nc.gpsimd.memset(v_pad[:], 0.0).then_inc(S["consts"], 1)
            nc.gpsimd.memset(state[:], 0.0).then_inc(S["consts"], 1)
            pool.wait_ge(S["consts"], CONSTS)

            def deviation(done, n, mv, ve, eps_, out, inner, count):
                need(pool, done, n + 1)
                nc.gpsimd.tensor_tensor(ve[:], mv[:, :, 1], eps_, ALU.add).then_inc(S[inner], 1)
                need(pool, inner, count)
                return nc.gpsimd.tensor_tensor(out, ve[:], minus_half[:], ALU.pow)

            def step(s, a, b, c, d):
                if c:
                    p, n = c.par, c.i
                    need(pool, "scale_done", n - 1)
                    deviation("stats2_done", n, mv2[:, p], ve2, eps[:, 1], rstd2[:, p], "pool_c", POOL_C * n + 1)\
                        .then_inc(S["rstd2_done"], 1)
                    need(pool, "high_done", n + 1)
                    need(pool, "y_done", 8 * (n - 1))
                    nc.gpsimd.tensor_tensor(x1_low[:, p], x1[:, p], x1_high[:, p].bitcast(F32), ALU.subtract)\
                        .then_inc(S["low_done"], 1)
                if a:
                    p, n = a.par, a.i
                    f = feat[:, p].rearrange("p u (s h d) -> p u s h d", s=2, d=HD)
                    need(pool, "feat_done", 2 * (n + 1))
                    nc.gpsimd.tensor_tensor(k_sum[:, :, 1], f[:, :, 1, 0], f[:, :, 1, 1], ALU.add)\
                        .then_inc(S["pool_a"], 1)
                    nc.gpsimd.tensor_copy(k_sum[:, :, 0], f[:, :, 1, 0]).then_inc(S["pool_a"], 1)
                    for h in range(2, HEADS):
                        need(pool, "pool_a", POOL_A * n + h)
                        nc.gpsimd.tensor_tensor(k_sum[:, :, h], k_sum[:, :, h - 1], f[:, :, 1, h], ALU.add)\
                            .then_inc(S["pool_a"], 1)
                    need(pool, "pool_a", POOL_A * (n + 1))
                    need(pool, "den_done", n)
                    nc.gpsimd.tensor_tensor(qk[:], k_sum[:].rearrange("p u h d -> p u (h d)"),
                                            feat[:, p, :, 0:128], ALU.mult).then_inc(S["qk_done"], 1)
                if c:
                    sum_experts(c, 0)
                if a:
                    need(pool, "den_done", n + 1)
                    need(pool, "qt_done", n)
                    need(pool, "pv_done", 2 * (n - 1))
                    nc.gpsimd.tensor_tensor(qn[:].rearrange("p u (h d) -> p u h d", d=HD),
                                            feat[:, p, :, 0:128].rearrange("p u (h d) -> p u h d", d=HD),
                                            rden[:].unsqueeze(3).broadcast_to([128, U, HEADS, HD]), ALU.mult)\
                        .then_inc(S["qn_done"], 1)
                if c:
                    sum_experts(c, 1)
                if a:
                    for e in range(2):
                        v = qkv[:, p, :, 256:384].rearrange("p u (g e d) -> p u g e d", e=2, d=HD)[:, :, :, e]
                        nc.gpsimd.tensor_copy(v_pad[:, p, :, e::2, HD * e:HD * e + HD], v)\
                            .then_inc(S["v_pad_done"], 1)
                if b:
                    need(pool, "kv_evac", b.i + 1)
                    need(pool, "inter_done", b.i + 1)
                    mine = state[:, U * b.par:U * b.par + U]
                    nc.gpsimd.tensor_tensor(mine, mine, kv_new[:], ALU.add).then_inc(S["state_done"], 1)
                if s:
                    need(pool, "qkv_done", U * (s.i - 1))
                    deviation("stats1_done", s.i, mv1[:, s.par], ve1, eps[:, 0], rstd1[:, s.par], "pool_s", s.i + 1)\
                        .then_inc(S["rstd1_done"], 1)
                if c:
                    sum_experts(c, 2)
                    sum_experts(c, 3)

            def sum_experts(c, u):
                n, s = c.i, u % 2
                need(pool, "y_act_done", U * n + u + 1)
                if u == 0:
                    need(pool, "out_done", n - 1)
                nc.gpsimd.tensor_tensor(y_act[:, s, 0:2], y_act[:, s, 0:2], y_act[:, s, 2:4], ALU.add)\
                    .then_inc(S["pool_y"], 1)
                need(pool, "pool_y", POOL_Y * n + 2 * u + 1)
                nc.gpsimd.tensor_tensor(y_sum[:, s], y_act[:, s, 0], y_act[:, s, 1], ALU.add)\
                    .then_inc(S["pool_y"], 1)
                need(pool, "pool_y", POOL_Y * n + 2 * u + 2)
                need(pool, "y_dve_done", U * n + u + 1)
                nc.gpsimd.tensor_tensor(y[:, c.par, u], y_sum[:, s], y_dve[:, s], ALU.add)\
                    .then_inc(S["y_sum_done"], 1)

            steps(pool, step)

        @block.scalar
        def _(act):
            def exponentials(a, h):
                need(act, "qkv_done", U * a.i + HALF_U * (h + 1))
                need(act, "feat_done", 2 * (a.i - 1) + h + 1)
                nc.scalar.activation(ex[:, 2 * h:2 * h + 2], qkv[:, a.par, 2 * h:2 * h + 2, 0:256], ACT.Exp,
                                     bias=-1.0).then_inc(S["ex_done"], 1)

            def expert_products(c, u):
                n, s = c.i, u % 2
                need(act, "y_done", 2 * (U * n + u) + 1)
                need(act, "y_sum_done", U * n + u - 1)
                for e in range(4):
                    last = nc.scalar.activation(y_act[:, s, e], big[2 * s][:, 128 * e:128 * e + 128], ACT.Copy,
                                                scale=scale[:, c.par, u, e:e + 1])
                last.then_inc(S["y_act_done"], 1)

            def step(s, a, b, c, d):
                if c:
                    need(act, "x1_done", c.i + 1)
                    need(act, "y_done", 8 * (c.i - 1))
                    nc.scalar.activation(x1_high[:, c.par], x1[:, c.par], ACT.Copy).then_inc(S["high_done"], 1)
                if a:
                    act.wait_ge(x_loaded[a.par], 16 * (a.half + 1))
                    need(act, "x1_done", a.i - 1)
                    nc.scalar.activation(x_res[:, a.par], x[:, a.par], ACT.Copy).then_inc(S["x_res_done"], 1)
                    exponentials(a, 0)
                if c:
                    need(act, "lgm_done", c.i + 1)
                    need(act, "coef_done", c.i)
                    nc.scalar.activation(pexp[:], lgm[:], ACT.Exp).then_inc(S["pexp_done"], 1)
                if a:
                    exponentials(a, 1)
                    p, n = a.par, a.i
                    need(act, "kt_done", n + 1)
                    need(act, "score_done", 8 * (n - 1))
                    for e, dst in ((0, k_even), (1, k_odd)):
                        nc.scalar.activation(dst[:, p].rearrange("p u t -> p (u t)"), bank_t[:], ACT.Copy,
                                             scale=parity[:, e:e + 1]).then_inc(S["k_evac"], 1)
                if c:
                    need(act, "scale_done", c.i + 1)
                    expert_products(c, 0)
                    expert_products(c, 1)
                if a:
                    need(act, "qt_done", a.i + 1)
                    need(act, "inter_done", a.i - 1)
                    nc.scalar.activation(q_t[:, a.par].rearrange("p u t -> p (u t)"), bank_q[:], ACT.Copy)\
                        .then_inc(S["q_evac"], 1)
                if c:
                    expert_products(c, 2)
                    need(act, "ct_done", c.i + 1)
                    need(act, "out_done", c.i - 1)
                    nc.scalar.activation(coef_t[:, c.par], bank_p[0:EXPERTS, :], ACT.Copy).then_inc(S["ct_evac"], 1)
                    expert_products(c, 3)

            act.wait_ge(S["setup_dve"], SETUP_DVE)
            steps(act, step)

        @block.vector
        def _(dve):
            done = [0]

            def setup(instruction):
                instruction.then_inc(S["setup_dve"], 1)
                done[0] += 1

            tt, stt = nc.vector.tensor_tensor, nc.vector.scalar_tensor_tensor
            dve.wait_ge(S["consts"], CONSTS)
            setup(nc.vector.tensor_scalar(centre[:], ident[:], -1.0 / CH, None, ALU.add))
            for e in range(2):
                first = heads_mask[:].rearrange("p (g e d) -> p e g d", e=2, d=HD)[:, e, :, 0]
                setup(nc.vector.reduce_sum(parity[:, e:e + 1], first, axis=AX))
            dve.wait_ge(S["w_loaded"], 16 * WEIGHTS)
            setup(nc.vector.tensor_scalar(b_qkv[:, 0:256], b_qkv[:, 0:256], 1.0, None, ALU.add))
            dve.wait_ge(S["setup_pe"], 1)
            setup(nc.vector.tensor_copy(w_t[:], bank_t[:, 0:384]))
            setup(nc.vector.tensor_copy(gamma_t[:], bank_p[:, 0:EXPERTS]))
            setup(nc.vector.tensor_copy(ins_mean[:], bank_q[:, 0:128]))
            dve.wait_ge(S["setup_pe"], 2)
            setup(nc.vector.tensor_copy(w_qkv[:], bank_t[:, 0:384]))
            setup(nc.vector.tensor_copy(gate_w[:], bank_p[:, 0:EXPERTS]))
            setup(nc.vector.tensor_copy(gamma_all[:], bank_q[:, 0:EXPERTS]))
            setup(nc.vector.tensor_copy(router_b[:], bank_n[:, 0:EXPERTS]))
            setup(nc.vector.tensor_copy(beta_t[:], big[2][:, 0:EXPERTS]))
            setup(nc.vector.tensor_copy(gamma_col[:], big[3][0:EXPERTS, 0:1]))
            dve.wait_ge(S["setup_dve"], done[0])
            for e in range(EXPERTS):
                setup(nc.vector.tensor_scalar(e_w[:, e], big[e // 4][:, 128 * (e % 4):128 * (e % 4) + 128],
                                              gamma_all[:, e:e + 1], None, ALU.mult))
            dve.wait_ge(S["setup_dve"], done[0])
            setup(nc.vector.tensor_copy(e_high[:], e_w[:]))
            dve.wait_ge(S["setup_dve"], done[0])
            setup(tt(e_low[:], e_w[:], e_high[:].bitcast(F32), ALU.subtract))
            dve.wait_ge(S["setup_pe"], 3)
            setup(stt(e_bias[:], e_bias_raw[:], gamma_col[:], bank_t[0:EXPERTS, 0:128], ALU.mult, ALU.add))
            assert done[0] == SETUP_DVE
            dve.wait_ge(S["setup_dve"], SETUP_DVE)

            def stats(bank, parts, out, chain, count):
                for u in range(U):
                    last = nc.vector.bn_stats(parts[:, u], bank[:, T * u:T * u + T])
                last.then_inc(S[chain], 1)
                need(dve, chain, count)
                nc.vector.memset(pause[:], 0.0)
                for u in range(U):
                    last = nc.vector.bn_aggr(out[:, u], parts[:, u])
                return last

            def causal(b, half, pairs):
                need(dve, "pv_done", 2 * (b.i - 1) + half + 1)
                for g in pairs:
                    need(dve, "score_done", 8 * b.i + 4 * half + g + 1)
                    tt(probs[:, half, g].rearrange("p u e t -> p (u e) t"),
                       big[g][:].rearrange("p (n t) -> p n t", t=T),
                       tri[:].unsqueeze(1).broadcast_to([128, 2 * HALF_U, T]), ALU.mult).then_inc(S["prob_done"], 1)

            def project(a, u):
                need(dve, "proj_done", U * a.i + u + 1)
                stt(qkv[:, a.par, u], (bank_p, bank_q)[u % 2][:, 0:384], rstd1[:, a.par, u:u + 1], b_qkv[:],
                    ALU.mult, ALU.add).then_inc(S["qkv_done"], 1)

            def features(a, h):
                need(dve, "ex_done", 2 * a.i + h + 1)
                stt(feat[:, a.par, 2 * h:2 * h + 2], ex[:, 2 * h:2 * h + 2], 1.0,
                    qkv[:, a.par, 2 * h:2 * h + 2, 0:256], ALU.min, ALU.max).then_inc(S["feat_done"], 1)

            def per_token(v):
                return v.unsqueeze(2).broadcast_to([128, U, EXPERTS])

            def route(c, n):
                p = c.par
                if n > 0:
                    need(dve, "dve_c", DVE_C * c.i + 1 + n)
                if n == 0:
                    need(dve, "logit_done", c.i + 1)
                    need(dve, "rstd2_done", c.i + 1)
                    i = tt(lg0[:], bank_t[:, 0:U * EXPERTS].rearrange("p (u e) -> p u e", u=U),
                           per_token(rstd2[:, p]), ALU.mult)
                    i.then_inc(S["lg_read"], 1)
                    need(dve, "lg_read", c.i + 1)
                    i = tt(lg[:], lg0[:], router_b[:].unsqueeze(1).broadcast_to([128, U, EXPERTS]), ALU.add)
                elif n == 1:
                    i = nc.vector.reduce_max(top[:, 0], lg[:], axis=AX)
                elif n == 2:
                    need(dve, "pexp_done", c.i)
                    i = tt(lgm[:], lg[:], per_token(top[:, 0]), ALU.subtract)
                    i.then_inc(S["lgm_done"], 1)
                    need(dve, "lgm_done", c.i + 1)
                    i = stt(rank[:, 0], lgm[:], 0.0, order[:], ALU.is_ge, ALU.mult)
                elif n == 3:
                    i = nc.vector.reduce_max(top[:, 1], rank[:, 0], axis=AX)
                elif n == 4:
                    i = tt(hot[:, 0], rank[:, 0], per_token(top[:, 1]), ALU.is_equal)
                elif n == 5:
                    i = stt(lg2[:], hot[:, 0], -BIG, lgm[:], ALU.mult, ALU.add)
                elif n == 6:
                    i = nc.vector.reduce_max(top[:, 2], lg2[:], axis=AX)
                elif n == 7:
                    i = tt(rank[:, 1], lg2[:], per_token(top[:, 2]), ALU.is_equal)
                elif n == 8:
                    i = tt(lg0[:], rank[:, 1], order[:], ALU.mult)
                elif n == 9:
                    i = nc.vector.reduce_max(top[:, 3], lg0[:], axis=AX)
                elif n == 10:
                    i = tt(hot[:, 1], lg0[:], per_token(top[:, 3]), ALU.is_equal)
                elif n == 11:
                    i = tt(hot[:, 2], hot[:, 0], hot[:, 1], ALU.add)
                elif n == 12:
                    need(dve, "pexp_done", c.i + 1)
                    i = nc.vector.reduce_sum(psum_[:, 0], pexp[:], axis=AX)
                elif n == 13:
                    i = nc.vector.reciprocal(psum_[:, 1], psum_[:, 0])
                elif n == 14:
                    i = tt(psel[:], pexp[:], hot[:, 2], ALU.mult)
                elif n == 15:
                    need(dve, "ct_done", c.i - 1)
                    tt(coef[:, p], psel[:], per_token(psum_[:, 1]), ALU.mult).then_inc(S["coef_done"], 1)
                    need(dve, "coef_done", c.i + 1)
                    need(dve, "y_act_done", U * (c.i - 1))
                    tt(scale[:, p], coef[:, p], per_token(rstd2[:, p]), ALU.mult).then_inc(S["scale_done"], 1)
                    return
                i.then_inc(S["dve_c"], 1)

            def weigh(c, u, e, count):
                s = u % 2
                out = big[2 * s + 1][:, 128 * e:128 * e + 128]
                w = scale[:, c.par, u, 4 + e:5 + e]
                if e == 0:
                    need(dve, "scale_done", c.i + 1)
                    need(dve, "y_done", 2 * (U * c.i + u) + 2)
                    need(dve, "y_sum_done", U * c.i + u - 1)
                    i = nc.vector.tensor_scalar(y_dve[:, s], out, w, None, ALU.mult)
                else:
                    need(dve, "dve_y", DVE_Y * c.i + count)
                    i = stt(y_dve[:, s], out, w, y_dve[:, s], ALU.mult, ALU.add)
                i.then_inc(S["y_dve_done" if e == 3 else "dve_y"], 1)

            def weigh_two(c):
                for e in range(4):
                    for u in range(2):
                        weigh(c, u, e, 2 * (e - 1) + u + 1)

            def routing(c, first, last):
                for n in range(first, last):
                    route(c, n)

            def residual(d):
                need(dve, "out_done", d.i + 1)
                if not isinstance(d.half, int) or d.half > 0:
                    dve.wait_ge(stored[d.par], 16 * d.half)
                tt(o[:, d.par].rearrange("p u t -> p (u t)"), bank_q[:],
                   x1[:, d.par].rearrange("p u t -> p (u t)"), ALU.add).then_inc(S["o_done"], 1)

            def denominators(a):
                need(dve, "qk_done", a.i + 1)
                nc.vector.reduce_sum(den[:], qk[:].rearrange("p u (h d) -> p u h d", d=HD), axis=AX)\
                    .then_inc(S["dve_a"], 1)
                need(dve, "dve_a", DVE_A * a.i + 1)
                nc.vector.tensor_scalar(den[:], den[:], 1e-10, None, ALU.add).then_inc(S["dve_a"], 1)
                need(dve, "dve_a", DVE_A * a.i + 2)
                need(dve, "qn_done", a.i)
                nc.vector.reciprocal(rden[:], den[:]).then_inc(S["den_done"], 1)

            def key_values(b):
                need(dve, "kv_done", b.i + 1)
                need(dve, "state_done", b.i)
                tt(kv_new[:], bank_p[:].rearrange("p (u d) -> p u d", u=U),
                   heads_mask[:].unsqueeze(1).broadcast_to([128, U, 128]), ALU.mult).then_inc(S["kv_evac"], 1)

            def attention(b):
                need(dve, "pv_done", 2 * (b.i + 1))
                need(dve, "x_res_done", b.i + 1)
                need(dve, "y_done", 8 * (b.i - 1))
                tt(x1[:, b.par].rearrange("p u t -> p (u t)"), bank_n[:],
                   x_res[:, b.par].rearrange("p u t -> p (u t)"), ALU.add).then_inc(S["x1_done"], 1)

            def step(s, a, b, c, d):
                if b:
                    causal(b, 0, (0,))
                if a:
                    need(dve, "rstd1_done", a.i + 1)
                    need(dve, "kv_done", a.i - 1)
                    need(dve, "v_pad_done", 2 * (a.i - 1))
                    project(a, 0)
                if c:
                    need(dve, "x1t_done", c.i + 1)
                    stats(bank_n, bn2, mv2[:, c.par], "dve_c", DVE_C * c.i + 1).then_inc(S["stats2_done"], 1)
                if b:
                    causal(b, 0, (1,))
                if a:
                    project(a, 1)
                if b:
                    causal(b, 0, (2,))
                if a:
                    need(dve, "qn_done", a.i - 1)
                    features(a, 0)
                    project(a, 2)
                if c:
                    routing(c, 0, 1)
                if b:
                    causal(b, 0, (3,))
                if c:
                    routing(c, 1, 3)
                if a:
                    project(a, 3)
                if c:
                    routing(c, 3, 7)
                if a:
                    features(a, 1)
                if c:
                    routing(c, 7, 16)
                if d:
                    residual(d)
                if c:
                    weigh_two(c)
                if b:
                    key_values(b)
                if a:
                    denominators(a)
                if b:
                    causal(b, 1, (0, 1))
                if s:
                    need(dve, "xt_done", s.i + 1)
                    stats(bank_t, bn, mv1[:, s.par], "dve_s", s.i + 1).then_inc(S["stats1_done"], 1)
                for g in range(2, PAIRS):
                    if b:
                        causal(b, 1, (g,))
                    if c:
                        weigh(c, 2, g - 2, 4 + g)
                if c:
                    weigh(c, 2, 2, 8)
                    weigh(c, 3, 0, None)
                    weigh(c, 2, 3, 9)
                    for e in range(1, 3):
                        weigh(c, 3, e, 9 + e)
                if b:
                    attention(b)
                if c:
                    weigh(c, 3, 3, 12)

            steps(dve, step)

        @block.tensor
        def _(pe):
            mm, transpose = nc.tensor.matmul, nc.tensor.transpose
            pe.wait_ge(S["consts"], CONSTS)
            pe.wait_ge(S["w_loaded"], 16 * WEIGHTS)
            for n in range(3):
                transpose(bank_t[:, 128 * n:128 * n + 128], w_raw[:, n], ident[:])
            transpose(bank_p[:, 0:EXPERTS], gamma_raw[:], ident[0:EXPERTS, 0:EXPERTS])
            mm(bank_q[:, 0:128], ins[:], mean_ins[:], start=True, stop=True).then_inc(S["setup_pe"], 1)
            pe.wait_ge(S["setup_dve"], 7)
            mm(bank_t[:, 0:384], centre[:], w_t[:], start=True, stop=True)
            mm(bank_p[:, 0:EXPERTS], centre[:], gate_raw[:], start=True, stop=True)
            mm(bank_q[:, 0:EXPERTS], ins_mean[:], gamma_t[:], start=True, stop=True)
            mm(bank_n[:, 0:EXPERTS], ins_mean[:], rmod[:], start=True, stop=True)
            for n in range(2):
                mm(big[n][:], centre[:], e_raw[:, 4 * n:4 * n + 4], start=True, stop=True)
            for e in range(EXPERTS):
                mm(big[2][:, e:e + 1], beta_raw[:, e], ins_mean[:, 0:1], start=True, stop=True)
            mm(big[3][0:EXPERTS, 0:1], gamma_t[:], ins_mean[:, 0:1], start=True, stop=True)\
                .then_inc(S["setup_pe"], 1)
            pe.wait_ge(S["setup_dve"], SETUP_DVE - 1)
            transpose(bank_t[0:EXPERTS, 0:128], beta_t[:], ident[:]).then_inc(S["setup_pe"], 1)
            pe.wait_ge(S["setup_dve"], SETUP_DVE)

            def scores(b, c, half, g):
                p = b.par
                if half == 0:
                    need(pe, "y_dve_done" if g % 2 else "y_act_done", U * (b.i - 1) - 1 + g // 2)
                    need(pe, "prob_done", 8 * b.i)
                elif c:
                    need(pe, "y_dve_done" if g % 2 else "y_act_done", U * c.i + 1 + g // 2)
                else:
                    need(pe, "prob_done", 8 * b.i + g + 1)
                rows = slice(32 * g, 32 * g + 32)
                for v in range(HALF_U):
                    u = HALF_U * half + v
                    for e, k in ((0, k_even), (1, k_odd)):
                        at = T * (2 * v + e)
                        last = mm(big[g][:, at:at + T], k[rows, p, u], q_t[rows, p, u], start=True, stop=True)
                last.then_inc(S["score_done"], 1)

            def values(b, half):
                p = b.par
                need(pe, "prob_done", 8 * b.i + 4 * (half + 1))
                for v in range(HALF_U):
                    u = HALF_U * half + v
                    for e in range(2):
                        for g in range(PAIRS):
                            last = mm(bank_n[32 * g:32 * g + 32, T * u:T * u + T], v_pad[:, p, u, 2 * g + e],
                                      probs[:, half, g, v, e], start=False, stop=(e == 1), skip_group_check=True)
                last.then_inc(S["pv_done"], 1)

            def project(a, u):
                mm((bank_p, bank_q)[u % 2][:, 0:384], x[:, a.par, u], w_qkv[:], start=True, stop=True)\
                    .then_inc(S["proj_done"], 1)

            def experts(b, c, u, half):
                bank = 2 * (u % 2) + half
                if b:
                    need(pe, "prob_done", 8 * b.i + 4 * (u // 2) + bank + 1)
                else:
                    need(pe, "y_dve_done" if half else "y_act_done", U * c.i + u - 1)
                w = slice(4 * half, 4 * half + 4)
                mm(big[bank][:], x1_high[:, c.par, u], e_high[:, w], start=True, stop=False)
                mm(big[bank][:], x1_high[:, c.par, u], e_low[:, w], start=False, stop=False)
                mm(big[bank][:], x1_low[:, c.par, u], e_high[:, w], start=False, stop=True)\
                    .then_inc(S["y_done"], 1)

            def x_transposed(s):
                pe.wait_ge(x_loaded[s.par], 16 * (s.half + 1))
                need(pe, "k_evac", 2 * s.i)
                for u in range(U):
                    last = transpose(bank_t[:, T * u:T * u + T], x[:, s.par, u], ident[:])
                last.then_inc(S["xt_done"], 1)

            def x1_transposed(c):
                need(pe, "x1_done", c.i + 1)
                for u in range(U):
                    last = transpose(bank_n[:, T * u:T * u + T], x1[:, c.par, u], ident[:])
                last.then_inc(S["x1t_done"], 1)

            def logits(a, c):
                if a:
                    need(pe, "stats1_done", a.i + 1)
                else:
                    need(pe, "lg_read", c.i)
                for u in range(U):
                    last = mm(bank_t[:, EXPERTS * u:EXPERTS * (u + 1)], x1[:, c.par, u], gate_w[:],
                              start=True, stop=True)
                last.then_inc(S["logit_done"], 1)

            def k_transposed(a, c):
                need(pe, "feat_done", 2 * (a.i + 1))
                if c:
                    need(pe, "lg_read", c.i + 1)
                for u in range(U):
                    last = transpose(bank_t[:, T * u:T * u + T], feat[:, a.par, u, 128:256], ident[:])
                last.then_inc(S["kt_done"], 1)

            def q_transposed(a, d):
                need(pe, "qn_done", a.i + 1)
                need(pe, "qkv_done", U * (a.i + 1))
                if d:
                    need(pe, "o_done", d.i + 1)
                for u in range(U):
                    last = transpose(bank_q[:, T * u:T * u + T], qn[:, u], ident[:])
                last.then_inc(S["qt_done"], 1)

            def output(a, b, d):
                p, n = d.par, d.i
                need(pe, "y_sum_done", U * (n + 1))
                need(pe, "ct_evac", n + 1)
                if a:
                    need(pe, "qkv_done", U * (a.i + 1))
                elif not b:
                    need(pe, "o_done", n)
                mm(bank_q[:], e_bias[:], coef_t[:, p], start=True, stop=False, skip_group_check=True)
                for u in range(U):
                    last = mm(bank_q[:, T * u:T * u + T], y[:, p, u], ident[:], start=False, stop=(u == U - 1),
                              skip_group_check=True)
                last.then_inc(S["out_done"], 1)

            def key_values(a, b, c):
                p = b.par
                if a:
                    need(pe, "qkv_done", U * a.i + 3)
                elif c:
                    need(pe, "ct_evac", c.i)
                for u in range(U):
                    last = mm(bank_p[:, 128 * u:128 * u + 128], feat[:, p, u, 128:256], qkv[:, p, u, 256:384],
                              start=True, stop=True)
                last.then_inc(S["kv_done"], 1)

            def from_state(b, c):
                p, n = b.par, b.i
                if c:
                    need(pe, "stats2_done", c.i + 1)
                need(pe, "state_done", n - 1)
                for u in range(U):
                    last = mm(bank_n[:, T * u:T * u + T], state[:, U * p + u], q_t[:, p, u],
                              start=(u == 0), stop=False, skip_group_check=True)
                last.then_inc(S["inter_done"], 1)
                need(pe, "v_pad_done", 2 * (n + 1))

            def coef_transposed(b, c):
                need(pe, "coef_done", c.i + 1)
                if b:
                    need(pe, "kv_evac", b.i + 1)
                else:
                    need(pe, "ct_evac", c.i)
                for u in range(U):
                    last = transpose(bank_p[0:EXPERTS, T * u:T * u + T], coef[:, c.par, u], ident[:])
                last.then_inc(S["ct_done"], 1)

            def step(s, a, b, c, d):
                if b:
                    need(pe, "k_evac", 2 * (b.i + 1))
                    need(pe, "q_evac", b.i + 1)
                for g in range(PAIRS):
                    if b:
                        scores(b, c, 0, g)
                    if a:
                        if g == 0:
                            need(pe, "rstd1_done", a.i + 1)
                            need(pe, "kv_evac", a.i - 1)
                            need(pe, "ct_evac", a.i - 2)
                        elif g == 1:
                            need(pe, "q_evac", a.i)
                        else:
                            need(pe, "qkv_done", U * a.i + g - 1)
                        project(a, g)
                    if c and g == 0:
                        x1_transposed(c)
                    if c and g == 2:
                        logits(a, c)
                if c:
                    need(pe, "low_done", c.i + 1)
                    experts(b, c, 0, 0)
                    experts(b, c, 0, 1)
                if d:
                    output(a, b, d)
                if c:
                    experts(b, c, 1, 0)
                if a:
                    k_transposed(a, c)
                if c:
                    experts(b, c, 1, 1)
                if b:
                    from_state(b, c)
                    values(b, 0)
                    key_values(a, b, c)
                    scores(b, c, 1, 0)
                if s:
                    x_transposed(s)
                if b:
                    scores(b, c, 1, 1)
                if c:
                    experts(b, c, 2, 0)
                if b:
                    scores(b, c, 1, 2)
                if c:
                    experts(b, c, 2, 1)
                if b:
                    scores(b, c, 1, 3)
                if a:
                    q_transposed(a, d)
                if c:
                    coef_transposed(b, c)
                    experts(b, c, 3, 0)
                    experts(b, c, 3, 1)
                if b:
                    values(b, 1)

            steps(pe, step)


_NAMES = ["x", "L0_conv_Wq", "L0_conv_bq", "L0_conv_Wkv", "L0_conv_bkv", "L0_ffn_Ins_tk", "L0_ffn_gate_w",
          "L0_ffn_expert_w", "L0_ffn_expert_b", "L0_ffn_gamma_w", "L0_ffn_beta_w", "L0_ffn_rmod_w"]


def kernel(**inputs):
    import numpy as np
    import concourse.bacc as bacc
    from concourse.bass_utils import run_bass_kernel_spmd

    nc = bacc.Bacc("TRN2", target_bir_lowering=False, num_devices=1)
    arrays, args = {}, []
    for name in _NAMES:
        a = np.ascontiguousarray(inputs[name])
        if name == "x":
            a = a.reshape(IMAGES, CH, TOKENS)
        arrays["in_" + name] = a
        args.append(nc.dram_tensor("in_" + name, a.shape, mybir.dt.from_np(a.dtype), kind="ExternalInput").ap())
    out = nc.dram_tensor("out", (IMAGES, CH, TOKENS), F32, kind="ExternalOutput").ap()
    program(nc, *args, out)
    result = run_bass_kernel_spmd(nc, [arrays], core_ids=[0])
    return result.results[0]["out"].reshape(IMAGES, CH, 48, 48)
```

```python
from contextlib import ExitStack

import concourse.bass as bass
from concourse import mybir

F32 = mybir.dt.float32
F32R = mybir.dt.float32r
ALU = mybir.AluOpType
ACT = mybir.ActivationFunctionType
AX = mybir.AxisListType.X

IMAGES, CH, TOKENS = 8, 128, 48 * 48
HEADS, HD = 8, 16
EXPERTS, INSTR = 8, 16
T = 128
U = 4
CHUNKS = TOKENS // T
PAR = IMAGES // U
GROUPS = PAR * CHUNKS
PAIRS = HEADS // 2
WIDE = T + EXPERTS
IN_N = 3
QUAD = 32
HALF_U = U // 2
BIG = 1.0e30

FIRST_WEIGHTS, REST_WEIGHTS = 5, 7
CONSTS = 3 + EXPERTS + 8
FIRST_DVE = 3 + 1 + 4
REST_DVE = 2 + 6 + EXPERTS + 2 + 4
POOL_A = HEADS - 1
POOL_C = 1
POOL_Y = 2 * U
DVE_A = 2
ROUTE = ("logits", "maximum", "ranks", "first rank", "largest", "others", "maximum of others", "sum of exp",
         "equal to it", "its reciprocal", "ranks of others", "softmax", "second rank", "scaled softmax",
         "second largest", "both")
DVE_C = 1 + len(ROUTE)
DVE_Y = 2 * U


class Group:

    def __init__(self, half, par):
        self.half, self.par, self.i = half, par, half * PAR + par


def program(nc, x_d, wq_d, bq_d, wkv_d, bkv_d, ins_d, gate_d, ew_d, eb_d, gamma_d, beta_d, rmod_d, out_d):
    ctx = ExitStack()
    with ctx:
        def sb(name, shape, dtype=F32):
            return ctx.enter_context(nc.sbuf_tensor(name, shape, dtype))

        def ps(name):
            return ctx.enter_context(nc.psum_tensor(name, [128, 512], F32))

        def sem(name):
            return ctx.enter_context(nc.semaphore(name))

        ident = sb("ident", [128, 128])
        tri = sb("tri", [128, T])
        heads_mask = sb("heads_mask", [128, 128])
        parity = sb("parity", [128, 2])
        order = sb("order", [128, U, EXPERTS])
        centre = sb("centre", [128, 128])
        mean_ins = sb("mean_ins", [INSTR, 128])
        minus_half = sb("minus_half", [128, U])
        w_raw = sb("w_raw", [128, 3, 128])
        w_t = sb("w_t", [128, 384])
        w_qkv = sb("w_qkv", [128, 384])
        w_high = sb("w_high", [128, 384], F32R)
        w_low = sb("w_low", [128, 384], F32R)
        b_qkv = sb("b_qkv", [128, 384])
        gate_raw = sb("gate_raw", [128, EXPERTS])
        id_gate = sb("id_gate", [128, WIDE])
        rmod = sb("rmod", [128, EXPERTS])
        router_b = sb("router_b", [128, EXPERTS])
        ins = sb("ins", [INSTR, 128])
        ins_mean = sb("ins_mean", [128, 128])
        gamma_raw = sb("gamma_raw", [EXPERTS, 128])
        gamma_t = sb("gamma_t", [128, EXPERTS])
        gamma_all = sb("gamma_all", [128, EXPERTS])
        gamma_col = sb("gamma_col", [EXPERTS, 1])
        beta_raw = sb("beta_raw", [128, EXPERTS, 128])
        beta_t = sb("beta_t", [128, EXPERTS])
        e_bias_raw = sb("e_bias_raw", [EXPERTS, 128])
        e_bias = sb("e_bias", [EXPERTS, 128])
        e_bias3 = sb("e_bias3", [3 * QUAD, 128], F32R)
        e_raw = sb("e_raw", [128, EXPERTS, 128])
        e_w = sb("e_w", [128, EXPERTS, 128])
        e_high = sb("e_high", [128, EXPERTS, 128], F32R)
        e_low = sb("e_low", [128, EXPERTS, 128], F32R)
        pause = sb("pause", [128, 1])
        eps = sb("eps", [128, 2, U])
        x = sb("x", [128, PAR, U, T])
        x_res = sb("x_res", [128, PAR, U, T])
        x_high = sb("x_high", [128, PAR, U, T], F32R)
        x_low = sb("x_low", [128, PAR, U, T], F32R)
        bn = sb("bn", [128, U, 6])
        mv1 = sb("mv1", [128, PAR, U, 2])
        ve1 = sb("ve1", [128, U])
        rstd1 = sb("rstd1", [128, PAR, U])
        qkv = sb("qkv", [128, PAR, U, 384])
        ex = sb("ex", [128, U, 256])
        feat = sb("feat", [128, PAR, U, 256])
        k_sum = sb("k_sum", [128, U, HEADS, HD])
        qk = sb("qk", [128, U, 128])
        den = sb("den", [128, U, HEADS])
        rden = sb("rden", [128, U, HEADS])
        qn = sb("qn", [128, U, 128])
        v_pad = sb("v_pad", [128, PAR, U, HEADS, 32])
        k_even = sb("k_even", [128, PAR, U, T])
        k_odd = sb("k_odd", [128, PAR, U, T])
        q_t = sb("q_t", [128, PAR, U, T])
        probs = sb("probs", [128, 2, PAIRS, HALF_U, 2, T])
        kv_new = sb("kv_new", [128, U, 128])
        state = sb("state", [128, IMAGES, 128])
        x1 = sb("x1", [128, PAR, U, T])
        x1_high = sb("x1_high", [128, PAR, U, T], F32R)
        x1_low = sb("x1_low", [128, PAR, U, T], F32R)
        bn2 = sb("bn2", [128, U, 6])
        mv2 = sb("mv2", [128, PAR, U, 2])
        ve2 = sb("ve2", [128, U])
        rstd2 = sb("rstd2", [128, PAR, U])
        lg_raw = sb("lg_raw", [128, U, EXPERTS])
        lg0 = sb("lg0", [128, U, EXPERTS])
        lg = sb("lg", [128, U, EXPERTS])
        lgm = sb("lgm", [128, U, EXPERTS])
        lg2 = sb("lg2", [128, U, EXPERTS])
        top = sb("top", [128, 4, U])
        rank = sb("rank", [128, 2, U, EXPERTS])
        hot = sb("hot", [128, 3, U, EXPERTS])
        pexp = sb("pexp", [128, U, EXPERTS])
        psum_ = sb("psum_", [128, 2, U])
        probs_e = sb("probs_e", [128, 2, U, EXPERTS])
        rank2 = sb("rank2", [128, U, EXPERTS])
        coef = sb("coef", [128, PAR, U, EXPERTS])
        scale = sb("scale", [128, PAR, U, EXPERTS])
        y_act = sb("y_act", [128, 2, 4, 128])
        y_one = sb("y_one", [128, 2, 128])
        y_dve = sb("y_dve", [128, 2, 128])
        y_sum = sb("y_sum", [128, 2, 128])
        y = sb("y", [128, PAR, U, 128])
        coef3 = sb("coef3", [128, PAR, U, 3 * QUAD], F32R)
        coef_t = sb("coef_t", [3 * QUAD, PAR, U * T], F32R)
        o = sb("o", [128, PAR, U, T])

        big = [ps(f"big{n}") for n in range(4)]
        bank_t = ps("bank_t")
        bank_p = ps("bank_p")
        bank_q = ps("bank_q")
        bank_n = ps("bank_n")

        names = ("consts setup first_loaded rest_loaded first_pe first_dve rest_pe rest_dve "
                 "xt_done x_high_done x_low_done x_res_done stats1_done rstd1_done proj_done qkv_done ex_done "
                 "feat_done k_first_done v_pad_done qk_done den_done qn_done kt_done k_evac qt_done q_evac "
                 "score_done prob_done kv_done kv_evac state_done inter_done pv_done x1_done "
                 "x1t_done high_done low_done lg_raw_done stats2_done rstd2_done lg_read lgm_done pexp_done "
                 "coef_done coef_high_done coef_low_done scale_done "
                 "y_done y_one_done y_act_done y_dve_done y_sum_done ct_done ct_evac out_done o_done "
                 "dve_s dve_a dve_c dve_y pool_s pool_a pool_c pool_y").split()
        S = {n: sem(n) for n in names}
        x_loaded = [sem(f"x_loaded{b}") for b in range(PAR)]
        stored = [sem(f"stored{b}") for b in range(PAR)]

        def dram(d, g):
            return d[U * g.par:U * g.par + U, :, bass.ds(g.half * T, T)].rearrange("n p t -> p n t")

        def need(eng, name, count):
            if not isinstance(count, int) or count > 0:
                eng.wait_ge(S[name], count)

        def is_first(g):
            return g is not None and isinstance(g.i, int) and g.i == 0

        def steps(eng, step):
            def grp(n):
                return Group(n // PAR, n % PAR) if 0 <= n < GROUPS else None

            first, last = 2, CHUNKS - 2
            for k in range(-2, PAR * first):
                step(grp(k + 2), grp(k + 1), grp(k), grp(k - 1), grp(k - 2))
            with eng.Fori(first, last) as t:
                step(Group(t + 1, 0), Group(t, 1), Group(t, 0), Group(t - 1, 1), Group(t - 1, 0))
                step(Group(t + 1, 1), Group(t + 1, 0), Group(t, 1), Group(t, 0), Group(t - 1, 1))
            for k in range(PAR * last, GROUPS + 2):
                step(grp(k + 2), grp(k + 1), grp(k), grp(k - 1), grp(k - 2))

        block = ctx.enter_context(nc.Block())

        @block.sync
        def _(sp):
            def load(g):
                need(sp, "xt_done", g.i - PAR + 1)
                need(sp, "x_low_done", g.i - PAR + 1)
                need(sp, "x_res_done", g.i - PAR + 1)
                sp.dma_start(x[:, g.par], dram(x_d, g)).then_inc(x_loaded[g.par], 16)

            load(Group(0, 0))
            weights = [
                (w_raw[:, 0], wq_d), (w_raw[:, 1], wkv_d[0:128]), (w_raw[:, 2], wkv_d[128:256]),
                (b_qkv[:, 0:128], bq_d.partition_broadcast(128)),
                (b_qkv[:, 128:384], bkv_d.partition_broadcast(128)),
                (gate_raw[:], gate_d), (rmod[:], rmod_d), (ins[:], ins_d[0]), (gamma_raw[:], gamma_d),
                (e_bias_raw[:], eb_d), (beta_raw[:], beta_d.rearrange("e h d -> h e d")),
                (e_raw[:], ew_d.rearrange("e l d -> l e d")),
            ]
            assert len(weights) == FIRST_WEIGHTS + REST_WEIGHTS
            for n, (dst, src) in enumerate(weights):
                sp.dma_start(dst, src).then_inc(S["first_loaded" if n < FIRST_WEIGHTS else "rest_loaded"], 16)
            load(Group(0, 1))

            def step(s, a, b, c, d):
                if d:
                    need(sp, "o_done", d.i + 1)
                    sp.dma_start(dram(out_d, d), o[:, d.par]).then_inc(stored[d.par], 16)
                if a:
                    ahead = Group(a.half + 1, a.par)
                    if not isinstance(ahead.i, int) or ahead.i < GROUPS:
                        load(ahead)

            steps(sp, step)
            for b in range(PAR):
                sp.wait_ge(stored[b], 16 * CHUNKS)

        @block.gpsimd
        def _(pool):
            nc.gpsimd.memset(ident[:], 0.0).then_inc(S["setup"], 1)
            nc.gpsimd.memset(tri[:], 1.0).then_inc(S["setup"], 1)
            nc.gpsimd.memset(heads_mask[:], 1.0).then_inc(S["setup"], 1)
            pool.wait_ge(S["setup"], 3)
            nc.gpsimd.affine_select(out=ident[:], in_=ident[:], compare_op=ALU.not_equal, fill=1.0, base=0,
                                    pattern=[[-1, 128]], channel_multiplier=1).then_inc(S["consts"], 1)
            nc.gpsimd.affine_select(out=tri[:], in_=tri[:], compare_op=ALU.is_ge, fill=0.0, base=0,
                                    pattern=[[1, T]], channel_multiplier=-1).then_inc(S["consts"], 1)
            blocks = heads_mask[:].rearrange("p (h d) -> p h d", d=HD)
            nc.gpsimd.affine_select(out=blocks, in_=blocks, compare_op=ALU.is_ge, fill=0.0, base=0,
                                    pattern=[[-HD, HEADS], [0, HD]], channel_multiplier=1).then_inc(S["setup"], 1)
            pool.wait_ge(S["setup"], 4)
            nc.gpsimd.affine_select(out=blocks, in_=blocks, compare_op=ALU.is_ge, fill=0.0, base=HD - 1,
                                    pattern=[[HD, HEADS], [0, HD]], channel_multiplier=-1).then_inc(S["consts"], 1)
            for e in range(EXPERTS):
                nc.gpsimd.memset(order[:, :, e:e + 1], float(EXPERTS - e)).then_inc(S["consts"], 1)
            nc.gpsimd.memset(mean_ins[:], 1.0 / INSTR).then_inc(S["consts"], 1)
            nc.gpsimd.memset(minus_half[:], -0.5).then_inc(S["consts"], 1)
            nc.gpsimd.memset(eps[:, 0], 1e-6).then_inc(S["consts"], 1)
            nc.gpsimd.memset(eps[:, 1], 1e-5).then_inc(S["consts"], 1)
            nc.gpsimd.memset(v_pad[:], 0.0).then_inc(S["consts"], 1)
            nc.gpsimd.memset(state[:], 0.0).then_inc(S["consts"], 1)
            nc.gpsimd.memset(coef3[:].bitcast(F32), 0.0).then_inc(S["consts"], 1)
            nc.gpsimd.memset(e_bias3[:].bitcast(F32), 0.0).then_inc(S["consts"], 1)
            pool.wait_ge(S["consts"], CONSTS)

            def deviation(done, n, mv, ve, eps_, out, inner, count):
                need(pool, done, n + 1)
                nc.gpsimd.tensor_tensor(ve[:], mv[:, :, 1], eps_, ALU.add).then_inc(S[inner], 1)
                need(pool, inner, count)
                return nc.gpsimd.tensor_tensor(out, ve[:], minus_half[:], ALU.pow)

            def step(s, a, b, c, d):
                if c:
                    p, n = c.par, c.i
                    need(pool, "scale_done", n - 1)
                    deviation("stats2_done", n, mv2[:, p], ve2, eps[:, 1], rstd2[:, p], "pool_c", POOL_C * n + 1)\
                        .then_inc(S["rstd2_done"], 1)
                if d:
                    sum_experts(d, 3)
                if c:
                    p, n = c.par, c.i
                    need(pool, "high_done", n + 1)
                    need(pool, "y_done", 8 * (n - 1))
                    nc.gpsimd.tensor_tensor(x1_low[:, p], x1[:, p], x1_high[:, p].bitcast(F32), ALU.subtract)\
                        .then_inc(S["low_done"], 1)
                if a:
                    p, n = a.par, a.i
                    f = feat[:, p].rearrange("p u (s h d) -> p u s h d", s=2, d=HD)
                    need(pool, "feat_done", 2 * (n + 1))
                    nc.gpsimd.tensor_tensor(k_sum[:, :, 1], f[:, :, 1, 0], f[:, :, 1, 1], ALU.add)\
                        .then_inc(S["pool_a"], 1)
                    for h in range(2, HEADS):
                        need(pool, "pool_a", POOL_A * n + h - 1)
                        nc.gpsimd.tensor_tensor(k_sum[:, :, h], k_sum[:, :, h - 1], f[:, :, 1, h], ALU.add)\
                            .then_inc(S["pool_a"], 1)
                    need(pool, "pool_a", POOL_A * (n + 1))
                    need(pool, "k_first_done", n + 1)
                    need(pool, "den_done", n)
                    nc.gpsimd.tensor_tensor(qk[:], k_sum[:].rearrange("p u h d -> p u (h d)"),
                                            feat[:, p, :, 0:128], ALU.mult).then_inc(S["qk_done"], 1)
                if c:
                    need(pool, "coef_high_done", c.i + 1)
                    nc.gpsimd.tensor_tensor(coef3[:, c.par, :, QUAD:QUAD + EXPERTS], coef[:, c.par],
                                            coef3[:, c.par, :, 0:EXPERTS].bitcast(F32), ALU.subtract)\
                        .then_inc(S["coef_low_done"], 1)
                if s:
                    need(pool, "x_high_done", s.i + 1)
                    need(pool, "proj_done", U * (s.i - 1))
                    nc.gpsimd.tensor_tensor(x_low[:, s.par], x[:, s.par], x_high[:, s.par].bitcast(F32),
                                            ALU.subtract).then_inc(S["x_low_done"], 1)
                if a:
                    need(pool, "den_done", n + 1)
                    need(pool, "qt_done", n)
                    nc.gpsimd.tensor_tensor(qn[:].rearrange("p u (h d) -> p u h d", d=HD),
                                            feat[:, p, :, 0:128].rearrange("p u (h d) -> p u h d", d=HD),
                                            rden[:].unsqueeze(3).broadcast_to([128, U, HEADS, HD]), ALU.mult)\
                        .then_inc(S["qn_done"], 1)
                if c:
                    sum_experts(c, 0)
                    sum_experts(c, 1)
                if s:
                    need(pool, "qkv_done", U * (s.i - 1))
                    deviation("stats1_done", s.i, mv1[:, s.par], ve1, eps[:, 0], rstd1[:, s.par], "pool_s", s.i + 1)\
                        .then_inc(S["rstd1_done"], 1)
                if b:
                    need(pool, "kv_evac", b.i + 1)
                    need(pool, "inter_done", b.i + 1)
                    mine = state[:, U * b.par:U * b.par + U]
                    nc.gpsimd.tensor_tensor(mine, mine, kv_new[:], ALU.add).then_inc(S["state_done"], 1)
                if c:
                    sum_experts(c, 2)

            def sum_experts(c, u):
                n, s = c.i, u % 2
                need(pool, "y_act_done", U * n + u + 1)
                if u == 0:
                    need(pool, "out_done", n - 1)
                nc.gpsimd.tensor_tensor(y_act[:, s, 0:2], y_act[:, s, 0:2], y_act[:, s, 2:4], ALU.add)\
                    .then_inc(S["pool_y"], 1)
                need(pool, "pool_y", POOL_Y * n + 2 * u + 1)
                nc.gpsimd.tensor_tensor(y_sum[:, s], y_act[:, s, 0], y_act[:, s, 1], ALU.add)\
                    .then_inc(S["pool_y"], 1)
                need(pool, "pool_y", POOL_Y * n + 2 * u + 2)
                need(pool, "y_dve_done", U * n + u + 1)
                nc.gpsimd.tensor_tensor(y[:, c.par, u], y_sum[:, s], y_dve[:, s], ALU.add)\
                    .then_inc(S["y_sum_done"], 1)

            steps(pool, step)

        @block.scalar
        def _(act):
            def exponentials(a, h):
                need(act, "qkv_done", U * a.i + HALF_U * (h + 1))
                need(act, "feat_done", 2 * (a.i - 1) + h + 1)
                nc.scalar.activation(ex[:, 2 * h:2 * h + 2], qkv[:, a.par, 2 * h:2 * h + 2, 0:256], ACT.Exp,
                                     bias=-1.0).then_inc(S["ex_done"], 1)

            def expert_products(c, u):
                n, s = c.i, u % 2
                need(act, "y_done", 2 * (U * n + u) + 2)
                need(act, "y_dve_done", U * n + u - 1)
                nc.scalar.activation(y_one[:, s], big[2 * s + 1][:, 0:128], ACT.Copy,
                                     scale=scale[:, c.par, u, 4:5]).then_inc(S["y_one_done"], 1)
                need(act, "y_sum_done", U * n + u - 1)
                for e in range(4):
                    last = nc.scalar.activation(y_act[:, s, e], big[2 * s][:, 128 * e:128 * e + 128], ACT.Copy,
                                                scale=scale[:, c.par, u, e:e + 1])
                last.then_inc(S["y_act_done"], 1)

            def step(s, a, b, c, d):
                if c:
                    need(act, "x1_done", c.i + 1)
                    need(act, "y_done", 8 * (c.i - 1))
                    nc.scalar.activation(x1_high[:, c.par], x1[:, c.par], ACT.Copy).then_inc(S["high_done"], 1)
                if a:
                    act.wait_ge(x_loaded[a.par], 16 * (a.half + 1))
                    need(act, "x1_done", a.i - 1)
                    nc.scalar.activation(x_res[:, a.par], x[:, a.par], ACT.Copy).then_inc(S["x_res_done"], 1)
                if b:
                    p = b.par
                    need(act, "qkv_done", U * (b.i + 1))
                    need(act, "pv_done", 2 * (b.i - 1))
                    for e in range(2):
                        v = qkv[:, p, :, 256:384].rearrange("p u (g e d) -> p u g e d", e=2, d=HD)[:, :, :, e]
                        nc.scalar.activation(v_pad[:, p, :, e::2, HD * e:HD * e + HD], v, ACT.Copy)\
                            .then_inc(S["v_pad_done"], 1)
                if c:
                    need(act, "stats2_done", c.i + 1)
                    need(act, "lg_read", c.i)
                    wide = bank_n[:, 0:WIDE * IN_N].rearrange("p (u t) -> p u t", t=WIDE)
                    nc.scalar.activation(lg_raw[:, 0:IN_N], wide[:, :, T:WIDE], ACT.Copy)\
                        .then_inc(S["lg_raw_done"], 1)
                    nc.scalar.activation(lg_raw[:, IN_N], bank_t[:, T:WIDE], ACT.Copy).then_inc(S["lg_raw_done"], 1)
                if a:
                    exponentials(a, 0)
                if c:
                    need(act, "lgm_done", c.i + 1)
                    need(act, "coef_done", c.i)
                    nc.scalar.activation(pexp[:], lgm[:], ACT.Exp).then_inc(S["pexp_done"], 1)
                if a:
                    exponentials(a, 1)
                    need(act, "feat_done", 2 * (a.i + 1))
                    need(act, "qk_done", a.i)
                    nc.scalar.activation(k_sum[:, :, 0], feat[:, a.par, :, 128:128 + HD], ACT.Copy)\
                        .then_inc(S["k_first_done"], 1)
                if a:
                    p, n = a.par, a.i
                    need(act, "kt_done", n + 1)
                    need(act, "score_done", 8 * (n - 1))
                    for e, dst in ((0, k_even), (1, k_odd)):
                        nc.scalar.activation(dst[:, p].rearrange("p u t -> p (u t)"), bank_t[:], ACT.Copy,
                                             scale=parity[:, e:e + 1]).then_inc(S["k_evac"], 1)
                if s:
                    act.wait_ge(x_loaded[s.par], 16 * (s.half + 1))
                    need(act, "proj_done", U * (s.i - 1))
                    nc.scalar.activation(x_high[:, s.par], x[:, s.par], ACT.Copy).then_inc(S["x_high_done"], 1)
                if c:
                    need(act, "coef_done", c.i + 1)
                    need(act, "ct_done", c.i - 1)
                    nc.scalar.activation(
                        coef3[:, c.par].rearrange("p u (s e) -> p u s e", e=QUAD)[:, :, 0::2, 0:EXPERTS],
                        coef[:, c.par].unsqueeze(2).broadcast_to([128, U, 2, EXPERTS]), ACT.Copy)\
                        .then_inc(S["coef_high_done"], 1)
                    need(act, "scale_done", c.i + 1)
                    expert_products(c, 0)
                    expert_products(c, 1)
                if a:
                    need(act, "qt_done", a.i + 1)
                    need(act, "inter_done", a.i - 1)
                    nc.scalar.activation(q_t[:, a.par].rearrange("p u t -> p (u t)"), bank_q[:], ACT.Copy)\
                        .then_inc(S["q_evac"], 1)
                if c:
                    expert_products(c, 2)
                    need(act, "ct_done", c.i + 1)
                    need(act, "out_done", c.i - 1)
                    nc.scalar.activation(coef_t[:, c.par], bank_p[0:3 * QUAD, :], ACT.Copy).then_inc(S["ct_evac"], 1)
                    expert_products(c, 3)

            act.wait_ge(S["consts"], CONSTS)
            act.wait_ge(S["first_dve"], FIRST_DVE)
            steps(act, step)

        @block.vector
        def _(dve):
            tt, stt = nc.vector.tensor_tensor, nc.vector.scalar_tensor_tensor

            def first_weights():
                dve.wait_ge(S["consts"], 3)
                nc.vector.tensor_scalar(centre[:], ident[:], -1.0 / CH, None, ALU.add).then_inc(S["first_dve"], 1)
                for e in range(2):
                    blocks = heads_mask[:].rearrange("p (g e d) -> p e g d", e=2, d=HD)[:, e, :, 0]
                    nc.vector.reduce_sum(parity[:, e:e + 1], blocks, axis=AX).then_inc(S["first_dve"], 1)
                dve.wait_ge(S["first_pe"], 1)
                nc.vector.tensor_copy(w_t[:], bank_t[:, 0:384]).then_inc(S["first_dve"], 1)
                dve.wait_ge(S["first_loaded"], 16 * FIRST_WEIGHTS)
                nc.vector.tensor_scalar(b_qkv[:, 0:256], b_qkv[:, 0:256], 1.0, None, ALU.add)\
                    .then_inc(S["first_dve"], 1)
                dve.wait_ge(S["first_pe"], 2)
                nc.vector.tensor_copy(w_qkv[:], bank_t[:, 0:384]).then_inc(S["first_dve"], 1)
                dve.wait_ge(S["first_dve"], 6)
                nc.vector.tensor_copy(w_high[:], w_qkv[:]).then_inc(S["first_dve"], 1)
                dve.wait_ge(S["first_dve"], 7)
                tt(w_low[:], w_qkv[:], w_high[:].bitcast(F32), ALU.subtract).then_inc(S["first_dve"], 1)
                dve.wait_ge(S["first_dve"], FIRST_DVE)

            def rest_of_weights():
                done = [0]

                def make(instruction):
                    instruction.then_inc(S["rest_dve"], 1)
                    done[0] += 1

                copy = nc.vector.tensor_copy
                dve.wait_ge(S["consts"], CONSTS)
                dve.wait_ge(S["rest_loaded"], 16 * REST_WEIGHTS)
                dve.wait_ge(S["rest_pe"], 1)
                make(copy(gamma_t[:], bank_n[:, 0:EXPERTS]))
                make(copy(ins_mean[:], bank_n[:, 128:256]))
                make(copy(id_gate[:, 0:T], ident[:]))
                dve.wait_ge(S["rest_pe"], 2)
                make(copy(id_gate[:, T:WIDE], big[2][:, 0:EXPERTS]))
                make(copy(gamma_all[:], big[2][:, EXPERTS:2 * EXPERTS]))
                make(copy(router_b[:], big[2][:, 2 * EXPERTS:3 * EXPERTS]))
                make(copy(beta_t[:], big[2][:, 3 * EXPERTS:4 * EXPERTS]))
                make(copy(gamma_col[:], big[3][0:EXPERTS, 0:1]))
                dve.wait_ge(S["rest_dve"], done[0])
                for e in range(EXPERTS):
                    make(nc.vector.tensor_scalar(e_w[:, e], big[e // 4][:, 128 * (e % 4):128 * (e % 4) + 128],
                                                 gamma_all[:, e:e + 1], None, ALU.mult))
                dve.wait_ge(S["rest_dve"], done[0])
                make(copy(e_high[:], e_w[:]))
                dve.wait_ge(S["rest_dve"], done[0])
                make(tt(e_low[:], e_w[:], e_high[:].bitcast(F32), ALU.subtract))
                dve.wait_ge(S["rest_pe"], 3)
                make(stt(e_bias[:], e_bias_raw[:], gamma_col[:], bank_n[0:EXPERTS, 0:128], ALU.mult, ALU.add))
                dve.wait_ge(S["rest_dve"], done[0])
                for n in range(2):
                    make(copy(e_bias3[QUAD * n:QUAD * n + EXPERTS], e_bias[:]))
                dve.wait_ge(S["rest_dve"], done[0])
                make(tt(e_bias3[2 * QUAD:2 * QUAD + EXPERTS], e_bias[:], e_bias3[0:EXPERTS].bitcast(F32),
                        ALU.subtract))
                assert done[0] == REST_DVE
                dve.wait_ge(S["rest_dve"], REST_DVE)

            def stats(units, parts, out, chain, count):
                for u in range(U):
                    last = nc.vector.bn_stats(parts[:, u], units[u])
                last.then_inc(S[chain], 1)
                need(dve, chain, count)
                nc.vector.memset(pause[:], 0.0)
                for u in range(U):
                    last = nc.vector.bn_aggr(out[:, u], parts[:, u])
                return last

            def causal(b, half, pairs):
                need(dve, "pv_done", 2 * (b.i - 1) + half + 1)
                for g in pairs:
                    need(dve, "score_done", 8 * b.i + 4 * half + g + 1)
                    tt(probs[:, half, g].rearrange("p u e t -> p (u e) t"),
                       big[g][:].rearrange("p (n t) -> p n t", t=T),
                       tri[:].unsqueeze(1).broadcast_to([128, 2 * HALF_U, T]), ALU.mult).then_inc(S["prob_done"], 1)

            def project(a, u):
                need(dve, "proj_done", U * a.i + u + 1)
                stt(qkv[:, a.par, u], (bank_p, bank_q)[u % 2][:, 0:384], rstd1[:, a.par, u:u + 1], b_qkv[:],
                    ALU.mult, ALU.add).then_inc(S["qkv_done"], 1)

            def features(a, h):
                need(dve, "ex_done", 2 * a.i + h + 1)
                stt(feat[:, a.par, 2 * h:2 * h + 2], ex[:, 2 * h:2 * h + 2], 1.0,
                    qkv[:, a.par, 2 * h:2 * h + 2, 0:256], ALU.min, ALU.max).then_inc(S["feat_done"], 1)

            def per_token(v):
                return v.unsqueeze(2).broadcast_to([128, U, EXPERTS])

            def route(c, name):
                p, n = c.par, c.i

                def after(earlier):
                    need(dve, "dve_c", DVE_C * n + 1 + ROUTE.index(earlier) + 1)

                if name == "product":
                    need(dve, "lg_raw_done", 2 * (n + 1))
                    need(dve, "rstd2_done", n + 1)
                    i = tt(lg0[:], lg_raw[:], per_token(rstd2[:, p]), ALU.mult)
                    i.then_inc(S["lg_read"], 1)
                    return
                elif name == "logits":
                    need(dve, "lg_read", n + 1)
                    i = tt(lg[:], lg0[:], router_b[:].unsqueeze(1).broadcast_to([128, U, EXPERTS]), ALU.add)
                elif name == "maximum":
                    after("logits")
                    i = nc.vector.reduce_max(top[:, 0], lg[:], axis=AX)
                elif name == "under":
                    after("maximum")
                    need(dve, "pexp_done", n)
                    i = tt(lgm[:], lg[:], per_token(top[:, 0]), ALU.subtract)
                    i.then_inc(S["lgm_done"], 1)
                    return
                elif name == "ranks":
                    need(dve, "lgm_done", n + 1)
                    i = stt(rank[:, 0], lgm[:], 0.0, order[:], ALU.is_ge, ALU.mult)
                elif name == "first rank":
                    after("ranks")
                    i = nc.vector.reduce_max(top[:, 1], rank[:, 0], axis=AX)
                elif name == "largest":
                    after("first rank")
                    i = tt(hot[:, 0], rank[:, 0], per_token(top[:, 1]), ALU.is_equal)
                elif name == "others":
                    after("largest")
                    i = stt(lg2[:], hot[:, 0], -BIG, lgm[:], ALU.mult, ALU.add)
                elif name == "maximum of others":
                    after("others")
                    i = nc.vector.reduce_max(top[:, 2], lg2[:], axis=AX)
                elif name == "equal to it":
                    after("maximum of others")
                    i = tt(rank[:, 1], lg2[:], per_token(top[:, 2]), ALU.is_equal)
                elif name == "ranks of others":
                    after("equal to it")
                    i = tt(rank2[:], rank[:, 1], order[:], ALU.mult)
                elif name == "second rank":
                    after("ranks of others")
                    i = nc.vector.reduce_max(top[:, 3], rank2[:], axis=AX)
                elif name == "second largest":
                    after("second rank")
                    i = tt(hot[:, 1], rank2[:], per_token(top[:, 3]), ALU.is_equal)
                elif name == "both":
                    after("second largest")
                    i = tt(hot[:, 2], hot[:, 0], hot[:, 1], ALU.add)
                elif name == "sum of exp":
                    need(dve, "pexp_done", n + 1)
                    i = nc.vector.reduce_sum(psum_[:, 0], pexp[:], axis=AX)
                elif name == "its reciprocal":
                    after("sum of exp")
                    i = nc.vector.reciprocal(psum_[:, 1], psum_[:, 0])
                elif name == "softmax":
                    after("its reciprocal")
                    i = tt(probs_e[:, 0], pexp[:], per_token(psum_[:, 1]), ALU.mult)
                elif name == "scaled softmax":
                    after("softmax")
                    i = tt(probs_e[:, 1], probs_e[:, 0], per_token(rstd2[:, p]), ALU.mult)
                elif name == "scale":
                    after("both")
                    need(dve, "y_act_done", U * (n - 1))
                    tt(scale[:, p], probs_e[:, 1], hot[:, 2], ALU.mult).then_inc(S["scale_done"], 1)
                    return
                elif name == "coef":
                    need(dve, "coef_low_done", n - 1)
                    tt(coef[:, p], probs_e[:, 0], hot[:, 2], ALU.mult).then_inc(S["coef_done"], 1)
                    return
                i.then_inc(S["dve_c"], 1)

            def weigh(c, u, e, count):
                s = u % 2
                out = big[2 * s + 1][:, 128 * (e + 1):128 * (e + 1) + 128]
                w = scale[:, c.par, u, 5 + e:6 + e]
                if e == 0:
                    need(dve, "scale_done", c.i + 1)
                    need(dve, "y_done", 2 * (U * c.i + u) + 2)
                    need(dve, "y_one_done", U * c.i + u + 1)
                    need(dve, "y_sum_done", U * c.i + u - 1)
                    so_far = y_one[:, s]
                else:
                    need(dve, "dve_y", DVE_Y * c.i + count)
                    so_far = y_dve[:, s]
                stt(y_dve[:, s], out, w, so_far, ALU.mult, ALU.add)\
                    .then_inc(S["y_dve_done" if e == 2 else "dve_y"], 1)

            def weigh_two(c):
                for e in range(3):
                    for u in range(2):
                        weigh(c, u, e, 2 * (e - 1) + u + 1)

            def routing(c, *names):
                for name in names:
                    route(c, name)

            def residual(d):
                need(dve, "out_done", d.i + 1)
                if not isinstance(d.half, int) or d.half > 0:
                    dve.wait_ge(stored[d.par], 16 * d.half)
                tt(o[:, d.par].rearrange("p u t -> p (u t)"), bank_q[:],
                   x1[:, d.par].rearrange("p u t -> p (u t)"), ALU.add).then_inc(S["o_done"], 1)

            def denominators(a):
                need(dve, "qk_done", a.i + 1)
                nc.vector.reduce_sum(den[:], qk[:].rearrange("p u (h d) -> p u h d", d=HD), axis=AX)\
                    .then_inc(S["dve_a"], 1)
                need(dve, "dve_a", DVE_A * a.i + 1)
                nc.vector.tensor_scalar(den[:], den[:], 1e-10, None, ALU.add).then_inc(S["dve_a"], 1)
                need(dve, "dve_a", DVE_A * a.i + 2)
                need(dve, "qn_done", a.i)
                nc.vector.reciprocal(rden[:], den[:]).then_inc(S["den_done"], 1)

            def key_values(b):
                need(dve, "kv_done", b.i + 1)
                need(dve, "state_done", b.i)
                tt(kv_new[:], bank_p[:].rearrange("p (u d) -> p u d", u=U),
                   heads_mask[:].unsqueeze(1).broadcast_to([128, U, 128]), ALU.mult).then_inc(S["kv_evac"], 1)

            def attention(b):
                need(dve, "pv_done", 2 * (b.i + 1))
                need(dve, "x_res_done", b.i + 1)
                need(dve, "y_done", 8 * (b.i - 1))
                tt(x1[:, b.par].rearrange("p u t -> p (u t)"), bank_n[:],
                   x_res[:, b.par].rearrange("p u t -> p (u t)"), ALU.add).then_inc(S["x1_done"], 1)

            def step(s, a, b, c, d):
                if b:
                    causal(b, 0, (0,))
                if a:
                    need(dve, "rstd1_done", a.i + 1)
                    need(dve, "kv_done", a.i - 1)
                    need(dve, "v_pad_done", 2 * (a.i - 1))
                    project(a, 0)
                if c:
                    need(dve, "x1t_done", c.i + 1)
                    units = [bank_n[:, WIDE * u:WIDE * u + T] for u in range(IN_N)] + [bank_t[:, 0:T]]
                    stats(units, bn2, mv2[:, c.par], "dve_c", DVE_C * c.i + 1).then_inc(S["stats2_done"], 1)
                if b:
                    causal(b, 0, (1,))
                if a:
                    project(a, 1)
                if b:
                    causal(b, 0, (2,))
                if a:
                    project(a, 2)
                if b:
                    causal(b, 0, (3,))
                if a:
                    need(dve, "qn_done", a.i - 1)
                    features(a, 0)
                if c:
                    routing(c, "product")
                if a:
                    project(a, 3)
                if c:
                    routing(c, "logits", "maximum", "under")
                if c:
                    routing(c, "ranks")
                if b:
                    causal(b, 1, (0,))
                if c:
                    routing(c, "first rank", "largest")
                if a:
                    features(a, 1)
                if is_first(a):
                    rest_of_weights()
                if c:
                    routing(c, "others")
                if b:
                    causal(b, 1, (1,))
                if c:
                    routing(c, "maximum of others", "sum of exp", "equal to it", "its reciprocal",
                            "ranks of others")
                if b:
                    key_values(b)
                if c:
                    routing(c, "softmax", "second rank", "scaled softmax", "second largest")
                if b:
                    causal(b, 1, (2,))
                if c:
                    routing(c, "both", "scale", "coef")
                if d:
                    residual(d)
                if b:
                    causal(b, 1, (3,))
                if a:
                    denominators(a)
                if c:
                    weigh_two(c)
                if s:
                    need(dve, "xt_done", s.i + 1)
                    units = [bank_t[:, T * u:T * u + T] for u in range(U)]
                    stats(units, bn, mv1[:, s.par], "dve_s", s.i + 1).then_inc(S["stats1_done"], 1)
                if b:
                    attention(b)
                if c:
                    weigh(c, 2, 0, None)
                    weigh(c, 2, 1, 5)
                    weigh(c, 3, 0, None)
                    weigh(c, 2, 2, 6)
                    weigh(c, 3, 1, 7)
                    weigh(c, 3, 2, 8)

            first_weights()
            steps(dve, step)

        @block.tensor
        def _(pe):
            mm, transpose = nc.tensor.matmul, nc.tensor.transpose

            def first_weights():
                pe.wait_ge(S["consts"], 1)
                pe.wait_ge(S["first_loaded"], 16 * FIRST_WEIGHTS)
                for n in range(3):
                    last = transpose(bank_t[:, 128 * n:128 * n + 128], w_raw[:, n], ident[:])
                last.then_inc(S["first_pe"], 1)
                pe.wait_ge(S["first_dve"], 4)
                mm(bank_t[:, 0:384], centre[:], w_t[:], start=True, stop=True).then_inc(S["first_pe"], 1)
                pe.wait_ge(S["first_dve"], FIRST_DVE)

            def rest_of_weights():
                pe.wait_ge(S["consts"], CONSTS)
                pe.wait_ge(S["rest_loaded"], 16 * REST_WEIGHTS)
                transpose(bank_n[:, 0:EXPERTS], gamma_raw[:], ident[0:EXPERTS, 0:EXPERTS])
                mm(bank_n[:, 128:256], ins[:], mean_ins[:], start=True, stop=True).then_inc(S["rest_pe"], 1)
                for n in range(2):
                    mm(big[n][:], centre[:], e_raw[:, 4 * n:4 * n + 4], start=True, stop=True)
                mm(big[2][:, 0:EXPERTS], centre[:], gate_raw[:], start=True, stop=True)
                pe.wait_ge(S["rest_dve"], 2)
                mm(big[2][:, EXPERTS:2 * EXPERTS], ins_mean[:], gamma_t[:], start=True, stop=True)
                mm(big[2][:, 2 * EXPERTS:3 * EXPERTS], ins_mean[:], rmod[:], start=True, stop=True)
                for e in range(EXPERTS):
                    at = 3 * EXPERTS + e
                    mm(big[2][:, at:at + 1], beta_raw[:, e], ins_mean[:, 0:1], start=True, stop=True)
                mm(big[3][0:EXPERTS, 0:1], gamma_t[:], ins_mean[:, 0:1], start=True, stop=True)\
                    .then_inc(S["rest_pe"], 1)
                pe.wait_ge(S["rest_dve"], 7)
                transpose(bank_n[0:EXPERTS, 0:128], beta_t[:], ident[:]).then_inc(S["rest_pe"], 1)

            def scores(b, half, g):
                p = b.par
                if half == 0:
                    need(pe, "y_dve_done" if g % 2 else "y_act_done", U * (b.i - 1) - 1 + g // 2)
                    need(pe, "prob_done", 8 * b.i)
                else:
                    need(pe, "prob_done", 8 * b.i + g + 1)
                rows = slice(32 * g, 32 * g + 32)
                for v in range(HALF_U):
                    u = HALF_U * half + v
                    for e, k in ((0, k_even), (1, k_odd)):
                        at = T * (2 * v + e)
                        last = mm(big[g][:, at:at + T], k[rows, p, u], q_t[rows, p, u], start=True, stop=True)
                last.then_inc(S["score_done"], 1)

            def values(b, half):
                p = b.par
                need(pe, "prob_done", 8 * b.i + 4 * (half + 1))
                for v in range(HALF_U):
                    u = HALF_U * half + v
                    for e in range(2):
                        for g in range(PAIRS):
                            last = mm(bank_n[32 * g:32 * g + 32, T * u:T * u + T], v_pad[:, p, u, 2 * g + e],
                                      probs[:, half, g, v, e], start=False, stop=(e == 1), skip_group_check=True)
                last.then_inc(S["pv_done"], 1)

            def project(a, u):
                out = (bank_p, bank_q)[u % 2][:, 0:384]
                mm(out, x_high[:, a.par, u], w_high[:], start=True, stop=False)
                mm(out, x_high[:, a.par, u], w_low[:], start=False, stop=False)
                mm(out, x_low[:, a.par, u], w_high[:], start=False, stop=True).then_inc(S["proj_done"], 1)

            def experts(b, c, u, half):
                bank = 2 * (u % 2) + half
                if b and u < 2:
                    need(pe, "prob_done", 8 * b.i + 4 + bank + 1)
                else:
                    need(pe, "y_dve_done" if half else "y_act_done", U * c.i + u - 1)
                w = slice(4 * half, 4 * half + 4)
                mm(big[bank][:], x1_high[:, c.par, u], e_high[:, w], start=True, stop=False)
                mm(big[bank][:], x1_high[:, c.par, u], e_low[:, w], start=False, stop=False)
                mm(big[bank][:], x1_low[:, c.par, u], e_high[:, w], start=False, stop=True)\
                    .then_inc(S["y_done"], 1)

            def x_transposed(s):
                pe.wait_ge(x_loaded[s.par], 16 * (s.half + 1))
                need(pe, "k_evac", 2 * s.i)
                for u in range(U):
                    last = transpose(bank_t[:, T * u:T * u + T], x[:, s.par, u], ident[:])
                last.then_inc(S["xt_done"], 1)

            def x1_transposed(a, c):
                need(pe, "x1_done", c.i + 1)
                if a:
                    need(pe, "stats1_done", a.i + 1)
                else:
                    need(pe, "lg_raw_done", 2 * c.i)
                for u in range(U):
                    out = bank_n[:, WIDE * u:WIDE * (u + 1)] if u < IN_N else bank_t[:, 0:WIDE]
                    last = mm(out, x1[:, c.par, u], id_gate[:], start=True, stop=True)
                last.then_inc(S["x1t_done"], 1)

            def k_transposed(a, c):
                need(pe, "feat_done", 2 * (a.i + 1))
                if c:
                    need(pe, "lg_raw_done", 2 * (c.i + 1))
                for u in range(U):
                    last = transpose(bank_t[:, T * u:T * u + T], feat[:, a.par, u, 128:256], ident[:])
                last.then_inc(S["kt_done"], 1)

            def q_transposed(a, d):
                need(pe, "qn_done", a.i + 1)
                need(pe, "qkv_done", U * (a.i + 1))
                if d:
                    need(pe, "o_done", d.i + 1)
                for u in range(U):
                    last = transpose(bank_q[:, T * u:T * u + T], qn[:, u], ident[:])
                last.then_inc(S["qt_done"], 1)

            def output(a, b, d):
                p, n = d.par, d.i
                need(pe, "y_sum_done", U * (n + 1))
                need(pe, "ct_evac", n + 1)
                if a:
                    need(pe, "qkv_done", U * (a.i + 1))
                elif not b:
                    need(pe, "o_done", n)
                mm(bank_q[:], e_bias3[:], coef_t[:, p], start=True, stop=False, skip_group_check=True)
                for u in range(U):
                    last = mm(bank_q[:, T * u:T * u + T], y[:, p, u], ident[:], start=False, stop=(u == U - 1),
                              is_transpose=True, skip_group_check=True)
                last.then_inc(S["out_done"], 1)

            def key_values(a, b, c):
                p = b.par
                if a:
                    need(pe, "qkv_done", U * a.i + 3)
                elif c:
                    need(pe, "ct_evac", c.i)
                for u in range(U):
                    last = mm(bank_p[:, 128 * u:128 * u + 128], feat[:, p, u, 128:256], qkv[:, p, u, 256:384],
                              start=True, stop=True)
                last.then_inc(S["kv_done"], 1)

            def from_state(b, c):
                p, n = b.par, b.i
                if c:
                    need(pe, "lg_raw_done", 2 * c.i + 1)
                need(pe, "state_done", n - 1)
                for u in range(U):
                    last = mm(bank_n[:, T * u:T * u + T], state[:, U * p + u], q_t[:, p, u],
                              start=(u == 0), stop=False, skip_group_check=True)
                last.then_inc(S["inter_done"], 1)
                need(pe, "v_pad_done", 2 * (n + 1))

            def coef_transposed(b, c):
                need(pe, "coef_low_done", c.i + 1)
                if b:
                    need(pe, "kv_evac", b.i + 1)
                else:
                    need(pe, "ct_evac", c.i)
                for u in range(U):
                    last = transpose(bank_p[0:3 * QUAD, T * u:T * u + T], coef3[:, c.par, u].bitcast(F32), ident[:])
                last.then_inc(S["ct_done"], 1)

            def step(s, a, b, c, d):
                if is_first(b):
                    pe.wait_ge(S["rest_dve"], REST_DVE)
                if b:
                    need(pe, "k_evac", 2 * (b.i + 1))
                    need(pe, "q_evac", b.i + 1)
                for g in range(PAIRS):
                    if b:
                        scores(b, 0, g)
                    if a:
                        if g == 0:
                            need(pe, "x_low_done", a.i + 1)
                            need(pe, "kv_evac", a.i - 1)
                            need(pe, "ct_evac", a.i - 2)
                        elif g == 1:
                            need(pe, "q_evac", a.i)
                        else:
                            need(pe, "qkv_done", U * a.i + g - 1)
                        project(a, g)
                    if c and g == 0:
                        x1_transposed(a, c)
                if is_first(a):
                    rest_of_weights()
                if b:
                    from_state(b, c)
                    scores(b, 1, 0)
                    values(b, 0)
                    scores(b, 1, 1)
                    key_values(a, b, c)
                    scores(b, 1, 2)
                if a:
                    k_transposed(a, c)
                if d:
                    output(a, b, d)
                if b:
                    scores(b, 1, 3)
                if c:
                    need(pe, "low_done", c.i + 1)
                    experts(b, c, 0, 0)
                    experts(b, c, 0, 1)
                    experts(b, c, 1, 0)
                if s:
                    x_transposed(s)
                if c:
                    experts(b, c, 1, 1)
                if b:
                    values(b, 1)
                if c:
                    experts(b, c, 2, 0)
                if a:
                    q_transposed(a, d)
                if c:
                    experts(b, c, 2, 1)
                    coef_transposed(b, c)
                    experts(b, c, 3, 0)
                    experts(b, c, 3, 1)

            first_weights()
            steps(pe, step)


_NAMES = ["x", "L0_conv_Wq", "L0_conv_bq", "L0_conv_Wkv", "L0_conv_bkv", "L0_ffn_Ins_tk", "L0_ffn_gate_w",
          "L0_ffn_expert_w", "L0_ffn_expert_b", "L0_ffn_gamma_w", "L0_ffn_beta_w", "L0_ffn_rmod_w"]


def kernel(**inputs):
    import numpy as np
    import concourse.bacc as bacc
    from concourse.bass_utils import run_bass_kernel_spmd

    nc = bacc.Bacc("TRN2", target_bir_lowering=False, num_devices=1)
    arrays, args = {}, []
    for name in _NAMES:
        a = np.ascontiguousarray(inputs[name])
        if name == "x":
            a = a.reshape(IMAGES, CH, TOKENS)
        arrays["in_" + name] = a
        args.append(nc.dram_tensor("in_" + name, a.shape, mybir.dt.from_np(a.dtype), kind="ExternalInput").ap())
    out = nc.dram_tensor("out", (IMAGES, CH, TOKENS), F32, kind="ExternalOutput").ap()
    program(nc, *args, out)
    result = run_bass_kernel_spmd(nc, [arrays], core_ids=[0])
    return result.results[0]["out"].reshape(IMAGES, CH, 48, 48)
```
